# Optimizing a Trainium2 kernel written in Bass

```python
import numpy as np
import jax
import jax.numpy as jnp

def _softmax(x, axis=-1):
    return jax.nn.softmax(x, axis=axis)

def _gelu(x):
    return jax.nn.gelu(x, approximate=True)

def _silu(x):
    return jax.nn.silu(x)

def _sigmoid(x):
    return jax.nn.sigmoid(x)

def _layernorm(x, axis=-1, eps=1e-05):
    m = jnp.mean(x, axis=axis, keepdims=True)
    v = jnp.var(x, axis=axis, keepdims=True)
    return (x - m) / jnp.sqrt(v + eps)

def _scatter_add(tgt, idx, src, axis=0):
    return tgt.at[idx].add(src)

def _segment_sum(src, seg, n):
    return jax.ops.segment_sum(src, seg, n)
kernel_name = 'mk_hybrid_d1_jaxref_r8_48b586'

def setup_inputs(seed: int=0):
    np.random.seed(seed)
    _w = jnp.asarray

    def _L0_attn_a_setup():
        import jax, jax.numpy as jnp
        import numpy as np
        DEPTH, DIM, DFF, VOCAB = (4, 64, 256, 512)
        EPS = 1e-05

        def layernorm(x, w, b):
            mu = jnp.mean(x, axis=-1, keepdims=True)
            var = jnp.mean((x - mu) ** 2, axis=-1, keepdims=True)
            return (x - mu) * jax.lax.rsqrt(var + EPS) * w + b

        def sconv(x, phazor_c, last_conv_c):
            B, L, D = x.shape
            r = jnp.abs(phazor_c)
            p = jnp.tanh(r) * jnp.exp(1j * jnp.angle(phazor_c))
            prog = p[None, :] ** jnp.arange(L, dtype=jnp.float32)[:, None]
            filt_fft = jnp.fft.fft(prog, n=2 * L, axis=0)
            x_fft = jnp.fft.fft(x.astype(jnp.complex64), n=2 * L, axis=1)
            conv = jnp.fft.ifft(filt_fft[None] * x_fft, axis=1)[:, :L]
            conv = conv + last_conv_c[None, None, :] * prog[None] * p[None, None, :]
            return conv.real.astype(x.dtype)

        def _forward(x, Win, bin, ln1_w, ln1_b, phz_re, phz_im, lc_re, lc_im, sc_lin, ln2_w, ln2_b, W1, b1, W2, b2, lnl_w, lnl_b, Wout, bout):
            h = jnp.einsum('blv,dv->bld', x, Win) + bin

            def body(h, p):
                l1w, l1b, pr, pi, lr, li, scl, l2w, l2b, w1, b1_, w2, b2_ = p
                y = jax.nn.silu(layernorm(h, l1w, l1b))
                y = sconv(y, pr + 1j * pi, lr + 1j * li)
                h = h + y * scl
                y = layernorm(h, l2w, l2b)
                y = jax.nn.silu(jnp.einsum('bld,fd->blf', y, w1) + b1_)
                y = jnp.einsum('blf,df->bld', y, w2) + b2_
                return (h + y, None)
            xs = (ln1_w, ln1_b, phz_re, phz_im, lc_re, lc_im, sc_lin, ln2_w, ln2_b, W1, b1, W2, b2)
            h, _ = jax.lax.scan(body, h, xs)
            h = layernorm(h, lnl_w, lnl_b)
            return jnp.einsum('bld,vd->blv', h, Wout) + bout
        key = jax.random.key(seed)
        ks = jax.random.split(key, 20)
        f32 = jnp.float32
        inp = {}
        inp['x'] = jax.random.normal(ks[0], (2, 512, VOCAB), dtype=f32)
        inp['Win'] = jax.random.normal(ks[1], (DIM, VOCAB), dtype=f32) * VOCAB ** (-0.5)
        inp['bin'] = jnp.zeros((DIM,), f32)
        inp['ln1_w'] = jnp.ones((DEPTH, DIM), f32)
        inp['ln1_b'] = jnp.zeros((DEPTH, DIM), f32)
        ang = 2 * np.pi * jnp.arange(DIM, dtype=f32) / DIM
        mag = jnp.abs(jax.random.normal(ks[2], (DEPTH, DIM), dtype=f32))
        inp['phz_re'] = mag * jnp.cos(ang)[None]
        inp['phz_im'] = mag * jnp.sin(ang)[None]
        inp['lc_re'] = jax.random.normal(ks[3], (DEPTH, DIM), dtype=f32)
        inp['lc_im'] = jax.random.normal(ks[4], (DEPTH, DIM), dtype=f32)
        inp['sc_lin'] = jnp.ones((DEPTH, DIM), f32)
        inp['ln2_w'] = jnp.ones((DEPTH, DIM), f32)
        inp['ln2_b'] = jnp.zeros((DEPTH, DIM), f32)
        inp['W1'] = jax.random.normal(ks[5], (DEPTH, DFF, DIM), dtype=f32) * DIM ** (-0.5)
        inp['b1'] = jnp.zeros((DEPTH, DFF), f32)
        inp['W2'] = jax.random.normal(ks[6], (DEPTH, DIM, DFF), dtype=f32) * DFF ** (-0.5)
        inp['b2'] = jnp.zeros((DEPTH, DIM), f32)
        inp['lnl_w'] = jnp.ones((DIM,), f32)
        inp['lnl_b'] = jnp.zeros((DIM,), f32)
        inp['Wout'] = jax.random.normal(ks[7], (VOCAB, DIM), dtype=f32) * DIM ** (-0.5)
        inp['bout'] = jnp.zeros((VOCAB,), f32)
        return inp
    _L0_attn_a_in = _L0_attn_a_setup()

    def _L0_attn_b_setup():
        import jax, jax.numpy as jnp
        import numpy as np
        import math
        B, S, DM = (1, 256, 512)
        H, HKV, HD = (32, 8, 128)
        EPS = 1e-06
        NEG_INF = -1e+30

        def _alibi_slopes(n_heads: int) -> np.ndarray:
            start = 2 ** (-2 ** (-(math.log2(n_heads) - 3)))
            return np.array([start * start ** i for i in range(n_heads)], dtype=np.float32)

        def _rmsnorm(t, w):
            tf = t.astype(jnp.float32)
            inv = jax.lax.rsqrt(jnp.mean(tf * tf, axis=-1, keepdims=True) + EPS)
            return (tf * inv * w).astype(t.dtype)
        key = jax.random.key(seed)
        ks = jax.random.split(key, 5)
        std = 0.02
        return {'x': jax.random.normal(ks[0], (B, S, DM), dtype=jnp.float32), 'Wq': jax.random.normal(ks[1], (H * HD, DM), dtype=jnp.float32) * std, 'Wk': jax.random.normal(ks[2], (HKV * HD, DM), dtype=jnp.float32) * std, 'Wv': jax.random.normal(ks[3], (HKV * HD, DM), dtype=jnp.float32) * std, 'Wo': jax.random.normal(ks[4], (H * HD, DM), dtype=jnp.float32).T * (std / math.sqrt(2 * 32)), 'q_norm_w': jnp.ones((HD,), dtype=jnp.float32), 'k_norm_w': jnp.ones((HD,), dtype=jnp.float32)}
    _L0_attn_b_in = _L0_attn_b_setup()

    def _L0_ffn_setup():
        import jax, jax.numpy as jnp
        import numpy as np
        B, S, H, I, R = (4, 32, 512, 1792, 4)

        def _anemll_linear(x, w, su, sv):
            w_eff = w * (su @ sv)
            return jnp.einsum('bsh,oh->bso', x, w_eff)
        key = jax.random.key(seed)
        ks = jax.random.split(key, 10)
        sd = 0.02
        return {'x': jax.random.normal(ks[0], (B, S, H), dtype=jnp.float32), 'gate_w': jax.random.normal(ks[1], (I, H), dtype=jnp.float32) * sd, 'gate_su': jax.random.normal(ks[2], (I, R), dtype=jnp.float32) * 0.5, 'gate_sv': jax.random.normal(ks[3], (R, H), dtype=jnp.float32) * 0.5, 'up_w': jax.random.normal(ks[4], (I, H), dtype=jnp.float32) * sd, 'up_su': jax.random.normal(ks[5], (I, R), dtype=jnp.float32) * 0.5, 'up_sv': jax.random.normal(ks[6], (R, H), dtype=jnp.float32) * 0.5, 'down_w': jax.random.normal(ks[7], (H, I), dtype=jnp.float32) * sd, 'down_su': jax.random.normal(ks[8], (H, R), dtype=jnp.float32) * 0.5, 'down_sv': jax.random.normal(ks[9], (R, I), dtype=jnp.float32) * 0.5}
    _L0_ffn_in = _L0_ffn_setup()
    _d = {'L0_attn_a_x': _L0_attn_a_in['x'], 'L0_attn_a_Win': _L0_attn_a_in['Win'], 'L0_attn_a_bin': _L0_attn_a_in['bin'], 'L0_attn_a_ln1_w': _L0_attn_a_in['ln1_w'], 'L0_attn_a_ln1_b': _L0_attn_a_in['ln1_b'], 'L0_attn_a_phz_re': _L0_attn_a_in['phz_re'], 'L0_attn_a_phz_im': _L0_attn_a_in['phz_im'], 'L0_attn_a_lc_re': _L0_attn_a_in['lc_re'], 'L0_attn_a_lc_im': _L0_attn_a_in['lc_im'], 'L0_attn_a_sc_lin': _L0_attn_a_in['sc_lin'], 'L0_attn_a_ln2_w': _L0_attn_a_in['ln2_w'], 'L0_attn_a_ln2_b': _L0_attn_a_in['ln2_b'], 'L0_attn_a_W1': _L0_attn_a_in['W1'], 'L0_attn_a_b1': _L0_attn_a_in['b1'], 'L0_attn_a_W2': _L0_attn_a_in['W2'], 'L0_attn_a_b2': _L0_attn_a_in['b2'], 'L0_attn_a_lnl_w': _L0_attn_a_in['lnl_w'], 'L0_attn_a_lnl_b': _L0_attn_a_in['lnl_b'], 'L0_attn_a_Wout': _L0_attn_a_in['Wout'], 'L0_attn_a_bout': _L0_attn_a_in['bout'], 'L0_attn_b_Wq': _L0_attn_b_in['Wq'], 'L0_attn_b_Wk': _L0_attn_b_in['Wk'], 'L0_attn_b_Wv': _L0_attn_b_in['Wv'], 'L0_attn_b_Wo': _L0_attn_b_in['Wo'], 'L0_attn_b_q_norm_w': _L0_attn_b_in['q_norm_w'], 'L0_attn_b_k_norm_w': _L0_attn_b_in['k_norm_w'], 'L0_ffn_gate_w': _L0_ffn_in['gate_w'], 'L0_ffn_gate_su': _L0_ffn_in['gate_su'], 'L0_ffn_gate_sv': _L0_ffn_in['gate_sv'], 'L0_ffn_up_w': _L0_ffn_in['up_w'], 'L0_ffn_up_su': _L0_ffn_in['up_su'], 'L0_ffn_up_sv': _L0_ffn_in['up_sv'], 'L0_ffn_down_w': _L0_ffn_in['down_w'], 'L0_ffn_down_su': _L0_ffn_in['down_su'], 'L0_ffn_down_sv': _L0_ffn_in['down_sv']}
    _x0 = _d['L0_attn_a_x']
    _d['L0_attn_a_x'] = jax.random.normal(jax.random.fold_in(jax.random.key(seed), 1), (8, 256, 512), dtype=_x0.dtype)
    del _x0
    return _d

def reference(L0_attn_a_x, L0_attn_a_Win, L0_attn_a_bin, L0_attn_a_ln1_w, L0_attn_a_ln1_b, L0_attn_a_phz_re, L0_attn_a_phz_im, L0_attn_a_lc_re, L0_attn_a_lc_im, L0_attn_a_sc_lin, L0_attn_a_ln2_w, L0_attn_a_ln2_b, L0_attn_a_W1, L0_attn_a_b1, L0_attn_a_W2, L0_attn_a_b2, L0_attn_a_lnl_w, L0_attn_a_lnl_b, L0_attn_a_Wout, L0_attn_a_bout, L0_attn_b_Wq, L0_attn_b_Wk, L0_attn_b_Wv, L0_attn_b_Wo, L0_attn_b_q_norm_w, L0_attn_b_k_norm_w, L0_ffn_gate_w, L0_ffn_gate_su, L0_ffn_gate_sv, L0_ffn_up_w, L0_ffn_up_su, L0_ffn_up_sv, L0_ffn_down_w, L0_ffn_down_su, L0_ffn_down_sv):

    def _L0_attn_a_ref(x, Win, bin, ln1_w, ln1_b, phz_re, phz_im, lc_re, lc_im, sc_lin, ln2_w, ln2_b, W1, b1, W2, b2, lnl_w, lnl_b, Wout, bout):
        import jax, jax.numpy as jnp
        import numpy as np
        DEPTH, DIM, DFF, VOCAB = (4, 64, 256, 512)
        EPS = 1e-05

        def layernorm(x, w, b):
            mu = jnp.mean(x, axis=-1, keepdims=True)
            var = jnp.mean((x - mu) ** 2, axis=-1, keepdims=True)
            return (x - mu) * jax.lax.rsqrt(var + EPS) * w + b

        def sconv(x, phazor_c, last_conv_c):
            B, L, D = x.shape
            r = jnp.abs(phazor_c)
            p = jnp.tanh(r) * jnp.exp(1j * jnp.angle(phazor_c))
            prog = p[None, :] ** jnp.arange(L, dtype=jnp.float32)[:, None]
            filt_fft = jnp.fft.fft(prog, n=2 * L, axis=0)
            x_fft = jnp.fft.fft(x.astype(jnp.complex64), n=2 * L, axis=1)
            conv = jnp.fft.ifft(filt_fft[None] * x_fft, axis=1)[:, :L]
            conv = conv + last_conv_c[None, None, :] * prog[None] * p[None, None, :]
            return conv.real.astype(x.dtype)

        def _forward(x, Win, bin, ln1_w, ln1_b, phz_re, phz_im, lc_re, lc_im, sc_lin, ln2_w, ln2_b, W1, b1, W2, b2, lnl_w, lnl_b, Wout, bout):
            h = jnp.einsum('blv,dv->bld', x, Win) + bin

            def body(h, p):
                l1w, l1b, pr, pi, lr, li, scl, l2w, l2b, w1, b1_, w2, b2_ = p
                y = jax.nn.silu(layernorm(h, l1w, l1b))
                y = sconv(y, pr + 1j * pi, lr + 1j * li)
                h = h + y * scl
                y = layernorm(h, l2w, l2b)
                y = jax.nn.silu(jnp.einsum('bld,fd->blf', y, w1) + b1_)
                y = jnp.einsum('blf,df->bld', y, w2) + b2_
                return (h + y, None)
            xs = (ln1_w, ln1_b, phz_re, phz_im, lc_re, lc_im, sc_lin, ln2_w, ln2_b, W1, b1, W2, b2)
            h, _ = jax.lax.scan(body, h, xs)
            h = layernorm(h, lnl_w, lnl_b)
            return jnp.einsum('bld,vd->blv', h, Wout) + bout
        return _forward(x, Win, bin, ln1_w, ln1_b, phz_re, phz_im, lc_re, lc_im, sc_lin, ln2_w, ln2_b, W1, b1, W2, b2, lnl_w, lnl_b, Wout, bout)

    def _L0_attn_b_ref(x, Wq, Wk, Wv, Wo, q_norm_w, k_norm_w):
        import jax, jax.numpy as jnp
        import numpy as np
        import math
        B, S, DM = (1, 256, 512)
        H, HKV, HD = (32, 8, 128)
        EPS = 1e-06
        NEG_INF = -1e+30

        def _alibi_slopes(n_heads: int) -> np.ndarray:
            start = 2 ** (-2 ** (-(math.log2(n_heads) - 3)))
            return np.array([start * start ** i for i in range(n_heads)], dtype=np.float32)

        def _rmsnorm(t, w):
            tf = t.astype(jnp.float32)
            inv = jax.lax.rsqrt(jnp.mean(tf * tf, axis=-1, keepdims=True) + EPS)
            return (tf * inv * w).astype(t.dtype)
        b, s, _ = x.shape
        G = H // HKV
        q = (x @ Wq.T).reshape(b, s, H, HD).transpose(0, 2, 1, 3)
        k = (x @ Wk.T).reshape(b, s, HKV, HD).transpose(0, 2, 1, 3)
        v = (x @ Wv.T).reshape(b, s, HKV, HD).transpose(0, 2, 1, 3)
        q = _rmsnorm(q, q_norm_w)
        k = _rmsnorm(k, k_norm_w)
        qg = q.reshape(b, HKV, G, s, HD)
        scores = jnp.einsum('bkgqd,bksd->bkgqs', qg, k) / math.sqrt(HD)
        slopes = jnp.asarray(_alibi_slopes(H)).reshape(HKV, G)
        pos = jnp.arange(s, dtype=jnp.float32)
        rel = pos[None, :] - pos[:, None]
        bias = jnp.where(rel > 0, NEG_INF, slopes[:, :, None, None] * rel)
        attn = jax.nn.softmax(scores + bias[None], axis=-1)
        out = jnp.einsum('bkgqs,bksd->bkgqd', attn, v)
        out = out.reshape(b, H, s, HD).transpose(0, 2, 1, 3).reshape(b, s, H * HD)
        return out @ Wo.T

    def _L0_ffn_ref(x, gate_w, gate_su, gate_sv, up_w, up_su, up_sv, down_w, down_su, down_sv):
        import jax, jax.numpy as jnp
        import numpy as np
        B, S, H, I, R = (4, 32, 512, 1792, 4)

        def _anemll_linear(x, w, su, sv):
            w_eff = w * (su @ sv)
            return jnp.einsum('bsh,oh->bso', x, w_eff)
        a = _anemll_linear(x, gate_w, gate_su, gate_sv)
        b = _anemll_linear(x, up_w, up_su, up_sv)
        d = jax.nn.silu(a) * b
        return _anemll_linear(d, down_w, down_su, down_sv)
    x = L0_attn_a_x
    x = x + _L0_attn_a_ref(_layernorm(x, axis=-1), L0_attn_a_Win, L0_attn_a_bin, L0_attn_a_ln1_w, L0_attn_a_ln1_b, L0_attn_a_phz_re, L0_attn_a_phz_im, L0_attn_a_lc_re, L0_attn_a_lc_im, L0_attn_a_sc_lin, L0_attn_a_ln2_w, L0_attn_a_ln2_b, L0_attn_a_W1, L0_attn_a_b1, L0_attn_a_W2, L0_attn_a_b2, L0_attn_a_lnl_w, L0_attn_a_lnl_b, L0_attn_a_Wout, L0_attn_a_bout)
    x = x + _L0_ffn_ref(_layernorm(x, axis=-1), L0_ffn_gate_w, L0_ffn_gate_su, L0_ffn_gate_sv, L0_ffn_up_w, L0_ffn_up_su, L0_ffn_up_sv, L0_ffn_down_w, L0_ffn_down_su, L0_ffn_down_sv)
    x = x + _L0_attn_b_ref(_layernorm(x, axis=-1), L0_attn_b_Wq, L0_attn_b_Wk, L0_attn_b_Wv, L0_attn_b_Wo, L0_attn_b_q_norm_w, L0_attn_b_k_norm_w)
    x = x + _L0_ffn_ref(_layernorm(x, axis=-1), L0_ffn_gate_w, L0_ffn_gate_su, L0_ffn_gate_sv, L0_ffn_up_w, L0_ffn_up_su, L0_ffn_up_sv, L0_ffn_down_w, L0_ffn_down_su, L0_ffn_down_sv)
    return x

_drawn_inputs = setup_inputs


def setup_inputs(seed=0):
    import zlib

    import numpy as np

    out = dict(_drawn_inputs(seed))
    spreads = {'L0_attn_a_bin': (0.0, 0.1),
     'L0_attn_a_ln1_w': (1.0, 0.2),
     'L0_attn_a_ln1_b': (0.0, 0.1),
     'L0_attn_a_sc_lin': (1.0, 0.2),
     'L0_attn_a_ln2_w': (1.0, 0.2),
     'L0_attn_a_ln2_b': (0.0, 0.1),
     'L0_attn_a_b1': (0.0, 0.1),
     'L0_attn_a_b2': (0.0, 0.1),
     'L0_attn_a_lnl_w': (1.0, 0.2),
     'L0_attn_a_lnl_b': (0.0, 0.1),
     'L0_attn_a_bout': (0.0, 0.1),
     'L0_attn_b_q_norm_w': (1.0, 0.2),
     'L0_attn_b_k_norm_w': (1.0, 0.2)}
    factors = {}
    for name, (base, spread) in spreads.items():
        noise = np.random.default_rng([zlib.crc32(name.encode()), seed]).standard_normal(out[name].shape)
        drawn = base * np.exp(spread * noise) if base else spread * noise
        out[name] = jnp.asarray(drawn.astype(out[name].dtype))
    for name, factor in factors.items():
        out[name] = (out[name] * factor).astype(out[name].dtype)
    return out
```

```python
from contextlib import ExitStack
import math

import numpy as np

import concourse.bass as bass
from concourse import mybir

F32 = mybir.dt.float32
F32R = mybir.dt.float32r
ALU = mybir.AluOpType
ACT = mybir.ActivationFunctionType
AX = mybir.AxisListType

P = 128
BATCH, SEQ, DM = 8, 256, 512
TOK = BATCH * SEQ
NT = TOK // P
KC = DM // P
BLK = 512
TPB = BLK // P
NBLK = TOK // BLK
DEPTH, DIM, DFF = 4, 64, 256
NG2 = P // DIM
HALVES = NT // (TPB * NG2)
INNER, RANK = 1792, 4
IC = INNER // P
HEADS, KVH, HD = 32, 8, 128
GRP = HEADS // KVH
STILES = SEQ // P
LN_EPS, RMS_EPS = 1e-5, 1e-6
NEG_INF = -1e30
SLOPE0 = 2 ** (-2 ** (-(math.log2(HEADS) - 3)))
SLOPES = [float(np.float32(SLOPE0 * SLOPE0 ** i)) for i in range(HEADS)]

VEC = {}
for _n, _w in (("ln1_w", DEPTH), ("ln1_b", DEPTH), ("phz_re", DEPTH), ("phz_im", DEPTH), ("lc_re", DEPTH),
               ("lc_im", DEPTH), ("sc_lin", DEPTH), ("ln2_w", DEPTH), ("ln2_b", DEPTH), ("b2", DEPTH),
               ("bin", 1), ("lnl_w", 1), ("lnl_b", 1)):
    VEC[_n] = (sum(w for _, w in VEC.values()), _w)
NVEC = sum(w for _, w in VEC.values())

PASSES = ((0, 0), (0, 1), (1, 0))


class Lane:

    def __init__(self, engine, sem):
        self.engine, self.sem, self.count, self.seen = engine, sem, 0, {}

    def wait(self, *tickets):
        for t in tickets:
            if t is None:
                continue
            if isinstance(t, list):
                self.wait(*t)
                continue
            sem, value = t
            if self.seen.get(id(sem), 0) < value:
                self.seen[id(sem)] = value
                self.engine.wait_ge(sem, value)

    def add(self, fn, *waits, mark=True):
        self.wait(*waits)
        ins = fn(self.engine)
        if not mark:
            return None
        ins.then_inc(self.sem, 1)
        self.count += 1
        return (self.sem, self.count)

    def now(self):
        return (self.sem, self.count) if self.count else None


class Slot:

    def __init__(self, sem):
        self.sem, self.count = sem, 0

    def dma(self, lane, dst, src, *waits):
        lane.wait(*waits)
        self.count += 16
        lane.engine.dma_start(dst, src).then_inc(self.sem, 16)
        return (self.sem, self.count)


def hybrid_block(nc, x_in, win, vecs, b1, w1, w2, wout, bout, ffn_w, lr_long, lr_short, wqkv, wo, qk_w, out, weff_dram):
    with ExitStack() as ctx:
        def sb(name, shape, dt=F32, stack=None):
            return (stack or ctx).enter_context(nc.sbuf_tensor(name, shape, dt))

        def sem(name):
            return ctx.enter_context(nc.semaphore(name))

        pe, act, dve, pool, sp = (Lane(engine, sem(name)) for engine, name in (
            (nc.tensor, "pe_done"), (nc.scalar, "act_done"), (nc.vector, "dve_done"), (nc.gpsimd, "pool_done"),
            (nc.sync, "sp_done")))
        psum = ctx.enter_context(nc.psum_tensor("psum", [P, 8, 512], F32))
        bank_free = [None] * 8

        x = sb("x", [P, NT, DM])
        ident = sb("ident", [P, P])
        mneg_half = sb("mneg_half", [P, 16])
        ln_mv = sb("ln_mv", [P, NT, 2])
        ln_bn = sb("ln_bn", [P, 2, 6])
        ln_var = sb("ln_var", [P, NT])
        ln_rstd = sb("ln_rstd", [P, NT])
        x_ready = [None] * NT

        def split(src, hi, lo, *ready, on=None):
            t_hi = act.add(lambda e: e.activation(hi, src, ACT.Copy), *ready)
            t_lo = dve.add(lambda e: e.tensor_tensor(lo, src, hi.bitcast(F32), ALU.subtract), t_hi, *ready)
            return t_lo

        def mm(out_ap, lhsT, rhs, start, stop, *waits, mark=False):
            return pe.add(lambda e: e.matmul(out_ap, lhsT, rhs, start=start, stop=stop), *waits, mark=mark)

        def mm3(out_ap, pairs, *waits, start=True, stop=True):
            pe.wait(*waits)
            n, last = 0, len(pairs) * len(PASSES) - 1
            for stat, mov in pairs:
                for a, b in PASSES:
                    t = mm(out_ap, stat[a], mov[b], start and n == 0, stop and n == last, mark=(n == last))
                    n += 1
            return t

        t_id0 = pool.add(lambda e: e.memset(ident[:], 0.0))
        t_ident = pool.add(lambda e: e.affine_select(out=ident[:], in_=ident[:], compare_op=ALU.not_equal, fill=1.0,
                                                     base=0, pattern=[[-1, P]], channel_multiplier=1), t_id0)
        t_half = pool.add(lambda e: e.memset(mneg_half[:], -0.5))

        def ln_stats(tiles):
            a, b = tiles[0], tiles[-1] + 1
            for t in tiles:
                t_bn = dve.add(lambda e, t=t: e.bn_stats(ln_bn[:, t % 2, :], x[:, t, :]), x_ready[t])
                t_mv = dve.add(lambda e, t=t: e.bn_aggr(ln_mv[:, t, :], ln_bn[:, t % 2, :]), t_bn)
            t_v = pool.add(lambda e: e.tensor_scalar(ln_var[:, a:b], ln_mv[:, a:b, 1], LN_EPS, None, ALU.add), t_mv)
            return pool.add(lambda e: e.tensor_tensor(ln_rstd[:, a:b], ln_var[:, a:b], mneg_half[:, 0:b - a], ALU.pow),
                            t_v, t_half)

        xn_users = [None, None]
        turn = {"xn": 0}

        def ln_apply(t, t_rstd, xn, bank, hi, lo, *dst_free):
            s = turn["xn"] % 2
            turn["xn"] += 1
            t_xn = dve.add(lambda e: e.tensor_scalar(xn[:, s, :], x[:, t, :], ln_mv[:, t, 0:1], ln_rstd[:, t:t + 1],
                                                     ALU.subtract, ALU.mult), t_rstd, xn_users[s])
            for k in range(KC):
                t_tr = pe.add(lambda e, k=k: e.transpose(psum[:, bank, k * P:(k + 1) * P], xn[:, s, k * P:(k + 1) * P],
                                                         ident[:]), t_xn, t_ident, bank_free[bank], mark=(k == KC - 1))
            xn_users[s] = t_tr
            src = psum[:, bank, :].rearrange("p (k c) -> p k c", k=KC)
            bank_free[bank] = split(src, hi, lo, t_tr, *dst_free)
            return bank_free[bank]

        def barrier():
            marks = [l.now() for l in (pe, act, dve, pool)]
            for l in (pe, act, dve, pool, sp):
                l.wait(*marks)

        phase1 = ExitStack()
        win_raw = sb("win_raw", [P, KC, DIM], F32, phase1)
        win_hi = sb("win_hi", [P, KC, 3 * DIM], F32R, phase1)
        win_lo = sb("win_lo", [P, KC, 3 * DIM], F32R, phase1)
        vec = sb("vec", [P, NVEC], F32, phase1)
        b1_sb = sb("b1_sb", [P, DEPTH, DFF // P], F32, phase1)
        w1_sb = sb("w1_sb", [P, DEPTH, DFF], F32, phase1)
        w2_sb = sb("w2_sb", [P, DEPTH * (DFF // P), 3 * DIM], F32, phase1)
        wout_sb = sb("wout_sb", [P, DM], F32, phase1)
        bout_sb = sb("bout_sb", [P, DM], F32, phase1)
        center = sb("center", [P, P], F32, phase1)
        blk_mean = sb("blk_mean", [P, NG2], F32, phase1)
        cosT = sb("cosT", [P, DEPTH, SEQ], F32, phase1)
        sinT = sb("sinT", [P, DEPTH, SEQ], F32, phase1)
        sm = sb("sm", [P, 32, DEPTH], F32, phase1)
        SW = BLK
        h = [sb(f"h{i}", [P, SW], F32, phase1) for i in range(HALVES)]
        cen = sb("cen", [P, SW], F32, phase1)
        act_y = sb("act_y", [P, SW], F32, phase1)
        zr = sb("zr", [P, SW], F32, phase1)
        zi = sb("zi", [P, SW], F32, phase1)
        ur = sb("ur", [P, SW], F32, phase1)
        ui = sb("ui", [P, SW], F32, phase1)
        rexp, sq, yn = ur, ui, zr
        sl = sb("sl", [P, NG2 * (DFF // P), SW], F32, phase1)
        svar = sb("svar", [P, TPB * NG2], F32, phase1)
        srstd = sb("srstd", [P, TPB * NG2], F32, phase1)

        def ffn_buffers(stack, tag):
            d = {}
            d["xn"] = sb(f"xn{tag}", [P, 2, DM], F32, stack)
            d["xT"] = [[sb(f"xT{s}{part}{tag}", [P, KC, BLK], F32R, stack) for part in "hl"] for s in range(2)]
            d["raw"] = sb(f"raw{tag}", [P, 2, 3 * DM], F32, stack)
            d["wgu"] = [[sb(f"wgu{s}{part}{tag}", [P, 2 * DM], F32R, stack) for part in "hl"] for s in range(2)]
            d["wdn"] = [[sb(f"wdn{s}{part}{tag}", [P, DM], F32R, stack) for part in "hl"] for s in range(3)]
            d["gate"] = sb(f"gate{tag}", [P, 2, BLK], F32, stack)
            d["d"] = sb(f"d{tag}", [P, BLK], F32, stack)
            d["dT"] = [[sb(f"dT{s}{part}{tag}", [P, BLK], F32R, stack) for part in "hl"] for s in range(2)]
            d["raw_slot"] = [Slot(sem(f"raw{s}{tag}")) for s in range(2)]
            d["xT_free"] = [None, None]
            return d

        F1 = ffn_buffers(phase1, "a")
        weff = sb("weff", [P, 3 * DM], F32, phase1)
        LR_ROWS = 3 * RANK
        long_raw = sl[:].rearrange("p n c -> p (n c)")[:, 0:INNER]
        short_raw = F1["raw"][:, 1, :].rearrange("p (n d) -> p n d", n=3)
        tab = F1["gate"][:, 0, :].rearrange("p (l t) -> p l t", l=DEPTH)
        tab2 = F1["gate"][:, 1, :].rearrange("p (l t) -> p l t", l=DEPTH)
        long_st = sb("long_st", [P, INNER], F32R, phase1)
        short_st = sb("short_st", [P, 3, DM], F32R, phase1)

        xv = x_in.rearrange("(t p) d -> p t d", p=P)
        for c in range(NBLK):
            t = Slot(sem(f"x_in{c}")).dma(sp, x[:, c * TPB:(c + 1) * TPB, :], xv[:, c * TPB:(c + 1) * TPB, :])
            for j in range(TPB):
                x_ready[c * TPB + j] = t
        t_zero_w2 = pool.add(lambda e: e.memset(w2_sb[:], 0.0))
        t_zero_long = dve.add(lambda e: e.memset(long_raw, 0.0))
        t_zero_short = dve.add(lambda e: e.memset(short_raw, 0.0))
        t_win = Slot(sem("win_in")).dma(sp, win_raw[:], win.rearrange("(k p) d -> p k d", p=P))
        s_small = Slot(sem("small_in"))
        for g in range(NG2):
            rows = slice(g * DIM, (g + 1) * DIM)
            s_small.dma(sp, vec[rows, :], vecs)
            s_small.dma(sp, w1_sb[rows, :, :], w1)
            s_small.dma(sp, wout_sb[rows, :], wout)
        s_small.dma(sp, b1_sb[:], b1)
        s_small.dma(sp, bout_sb[:], bout.partition_broadcast(P))
        t_small = s_small.dma(sp, w2_sb[:, :, DIM:2 * DIM], w2, t_zero_w2)
        s_lr = Slot(sem("lr_in"))
        for q in range(3):
            s_lr.dma(sp, long_raw[32 * q:32 * q + LR_ROWS, :], lr_long, t_zero_long)
            for kind in range(3):
                r = 32 * q + RANK * kind
                t_lr = s_lr.dma(sp, short_raw[r:r + RANK, kind, :], lr_short[RANK * kind:RANK * (kind + 1), :],
                                t_zero_short)

        t_wz0 = dve.add(lambda e: e.memset(win_hi[:].bitcast(F32), 0.0))
        t_wz1 = dve.add(lambda e: e.memset(win_lo[:].bitcast(F32), 0.0))
        t_winr = split(win_raw[:], win_hi[:, :, DIM:2 * DIM], win_lo[:, :, DIM:2 * DIM], t_win, t_wz0, t_wz1)

        t_c = pool.add(lambda e: e.memset(blk_mean[:], 0.0))
        t_c = pool.add(lambda e: e.memset(center[:], 0.0), t_c)
        for g in range(NG2):
            rows = slice(g * DIM, (g + 1) * DIM)
            pool.add(lambda e, r=rows, g=g: e.memset(blk_mean[r, g:g + 1], 1.0 / DIM), t_c)
            t_c2 = pool.add(lambda e, r=rows: e.memset(center[r, r], -1.0 / DIM), t_c)
        t_center = pool.add(lambda e: e.tensor_tensor(center[:], center[:], ident[:], ALU.add), t_c2, t_ident)

        def col(name, layer=None):
            a, w = VEC[name]
            return vec[:, a:a + w] if layer is None else vec[:, a + layer:a + layer + 1]

        cols = {n: i for i, n in enumerate(("m", "a", "b", "q", "z", "ri", "c1", "s1", "r", "rho", "t0", "t1", "t2",
                                            "mt", "za", "zb", "pc", "ps", "pc2", "ps2", "absi"))}

        def C(n):
            return sm[:, cols[n], :]

        chain = [dve.add(lambda e: e.memset(sm[:], 0.0))]

        def step(lane, fn):
            chain[0] = lane.add(fn, chain[0])
            return chain[0]

        dve.wait(t_small)
        pool.wait(t_small)
        step(dve, lambda e: e.tensor_scalar(C("m"), col("phz_re"), -1.0, None, ALU.mult))
        step(dve, lambda e: e.tensor_tensor(C("m"), C("m"), col("phz_re"), ALU.max))
        step(dve, lambda e: e.tensor_scalar(C("absi"), col("phz_im"), -1.0, None, ALU.mult))
        step(dve, lambda e: e.tensor_tensor(C("absi"), C("absi"), col("phz_im"), ALU.max))
        step(dve, lambda e: e.tensor_tensor(C("m"), C("m"), C("absi"), ALU.max))
        step(dve, lambda e: e.tensor_scalar(C("m"), C("m"), 1e-30, None, ALU.max))
        step(dve, lambda e: e.reciprocal(C("t0"), C("m")))
        step(dve, lambda e: e.tensor_tensor(C("a"), col("phz_re"), C("t0"), ALU.mult))
        step(dve, lambda e: e.tensor_tensor(C("b"), col("phz_im"), C("t0"), ALU.mult))
        step(dve, lambda e: e.tensor_tensor(C("q"), C("a"), C("a"), ALU.mult))
        step(dve, lambda e: e.tensor_tensor(C("t1"), C("b"), C("b"), ALU.mult))
        step(dve, lambda e: e.tensor_tensor(C("q"), C("q"), C("t1"), ALU.add))
        step(dve, lambda e: e.tensor_scalar(C("z"), C("q"), 0.0, None, ALU.is_equal))
        step(dve, lambda e: e.tensor_tensor(C("q"), C("q"), C("z"), ALU.add))
        step(dve, lambda e: e.tensor_tensor(C("a"), C("a"), C("z"), ALU.add))
        step(pool, lambda e: e.tensor_tensor(C("ri"), C("q"), mneg_half[:, 0:DEPTH], ALU.pow))
        step(dve, lambda e: e.tensor_tensor(C("t0"), C("ri"), C("ri"), ALU.mult))
        step(dve, lambda e: e.tensor_tensor(C("t0"), C("t0"), C("q"), ALU.mult))
        step(dve, lambda e: e.tensor_scalar(C("t0"), C("t0"), -0.5, 1.5, ALU.mult, ALU.add))
        step(dve, lambda e: e.tensor_tensor(C("ri"), C("ri"), C("t0"), ALU.mult))
        step(dve, lambda e: e.tensor_tensor(C("c1"), C("a"), C("ri"), ALU.mult))
        step(dve, lambda e: e.tensor_tensor(C("s1"), C("b"), C("ri"), ALU.mult))
        step(dve, lambda e: e.tensor_tensor(C("r"), C("q"), C("ri"), ALU.mult))
        step(dve, lambda e: e.tensor_tensor(C("r"), C("r"), C("m"), ALU.mult))
        step(act, lambda e: e.activation(C("rho"), C("r"), ACT.Tanh))
        step(dve, lambda e: e.tensor_tensor(C("t0"), C("c1"), col("lc_re"), ALU.mult))
        step(dve, lambda e: e.tensor_tensor(C("t1"), C("s1"), col("lc_im"), ALU.mult))
        step(dve, lambda e: e.tensor_tensor(C("za"), C("t0"), C("t1"), ALU.subtract))
        step(dve, lambda e: e.tensor_tensor(C("t0"), C("c1"), col("lc_im"), ALU.mult))
        step(dve, lambda e: e.tensor_tensor(C("t1"), C("s1"), col("lc_re"), ALU.mult))
        step(dve, lambda e: e.tensor_tensor(C("zb"), C("t0"), C("t1"), ALU.add))
        step(dve, lambda e: e.tensor_scalar(C("zb"), C("zb"), -1.0, None, ALU.mult))
        t_state = chain[0]
        step(pool, lambda e: e.memset(cosT[:, :, 0:1], 1.0))
        step(pool, lambda e: e.memset(sinT[:, :, 0:1], 0.0))
        step(pool, lambda e: e.tensor_copy(C("pc"), C("c1")))
        step(pool, lambda e: e.tensor_copy(C("ps"), C("s1")))
        n = 1
        while n < SEQ:
            def wide(name, n=n):
                return sm[:, cols[name], :].rearrange("p (l o) -> p l o", o=1).broadcast_to([P, DEPTH, n])
            c0, s0 = cosT[:, :, 0:n], sinT[:, :, 0:n]
            c1, s1 = cosT[:, :, n:2 * n], sinT[:, :, n:2 * n]
            ta, tb = tab[:, :, 0:n], tab2[:, :, 0:n]
            before = chain[0]
            p1 = pool.add(lambda e, c1=c1, c0=c0, w=wide: e.tensor_tensor(c1, c0, w("pc"), ALU.mult), before)
            p2 = pool.add(lambda e, ta=ta, s0=s0, w=wide: e.tensor_tensor(ta, s0, w("ps"), ALU.mult), before)
            p3 = pool.add(lambda e, s1=s1, s0=s0, w=wide: e.tensor_tensor(s1, s0, w("pc"), ALU.mult), before)
            p4 = pool.add(lambda e, tb=tb, c0=c0, w=wide: e.tensor_tensor(tb, c0, w("ps"), ALU.mult), before)
            pool.add(lambda e, c1=c1, ta=ta: e.tensor_tensor(c1, c1, ta, ALU.subtract), p2)
            chain[0] = pool.add(lambda e, s1=s1, tb=tb: e.tensor_tensor(s1, s1, tb, ALU.add), p4)
            n *= 2
            if n < SEQ:
                step(pool, lambda e: e.tensor_tensor(C("pc2"), C("pc"), C("pc"), ALU.mult))
                step(pool, lambda e: e.tensor_tensor(C("t1"), C("ps"), C("ps"), ALU.mult))
                step(pool, lambda e: e.tensor_tensor(C("ps2"), C("pc"), C("ps"), ALU.mult))
                step(pool, lambda e: e.tensor_tensor(C("pc"), C("pc2"), C("t1"), ALU.subtract))
                step(pool, lambda e: e.tensor_tensor(C("ps"), C("ps2"), C("ps2"), ALU.add))
        t_tables = chain[0]

        t_l = act.add(lambda e: e.activation(long_st[0:96, :], long_raw[0:96, :], ACT.Copy), t_lr)
        t_s = act.add(lambda e: e.activation(short_st[0:96, :, :], short_raw[0:96, :, :], ACT.Copy), t_lr)
        dve.add(lambda e: e.tensor_tensor(long_st[32:64, :], long_raw[32:64, :], long_st[32:64, :].bitcast(F32),
                                          ALU.subtract), t_l)
        t_lowrank = dve.add(lambda e: e.tensor_tensor(short_st[64:96, :, :], short_raw[64:96, :, :],
                                                      short_st[64:96, :, :].bitcast(F32), ALU.subtract), t_s)

        free = {}
        free["sl"] = t_lowrank

        def stack_half(half, banks):
            turn_b = [0]

            def bank():
                turn_b[0] += 1
                return banks[turn_b[0] % len(banks)]

            hh = h[half]
            tiles = list(range(half * TPB * NG2, (half + 1) * TPB * NG2))
            for g in range(NG2):
                rs = ln_stats(tiles[g * TPB:(g + 1) * TPB])
                yield
                xT = F1["xT"][g]
                for j in range(TPB):
                    t = tiles[g * TPB + j]
                    cols_ = slice(j * P, (j + 1) * P)
                    t_x = ln_apply(t, rs, F1["xn"], bank(), xT[0][:, :, cols_], xT[1][:, :, cols_], F1["xT_free"][g])
                    x_ready[t] = pool.add(lambda e, t=t: e.tensor_tensor(x[:, t, :], x[:, t, :], bout_sb[:], ALU.add),
                                          t_x, t_small)
                    yield
                if g == 0:
                    bw = bank()
                    rest = [b for b in banks if b != bw]
                    banks_all, banks[:] = list(banks), rest
                w_off = DIM * (NG2 - 1 - g)
                pairs = [((win_hi[:, k, w_off:w_off + P], win_lo[:, k, w_off:w_off + P]),
                          (xT[0][:, k, :], xT[1][:, k, :])) for k in range(KC)]
                t_h = mm3(psum[:, bw, :], pairs, t_x, t_winr, bank_free[bw], start=(g == 0), stop=(g == NG2 - 1))
                F1["xT_free"][g] = t_h
                yield
            banks[:] = banks_all
            t_h = dve.add(lambda e: e.tensor_scalar(hh[:], psum[:, bw, :], col("bin"), None, ALU.add), t_h)
            bank_free[bw] = t_h

            def norm(t_h):
                b = bank()
                t_c = mm(psum[:, b, :], center[:], hh[:], True, True, t_h, t_center, bank_free[b], mark=True)
                t_cc = dve.add(lambda e: e.tensor_copy(cen[:], psum[:, b, :]), t_c, free.get("cen"))
                t_sq = act.add(lambda e: e.activation(sq[:], psum[:, b, :], ACT.Square), t_cc, free.get("ui"))
                bank_free[b] = t_sq
                yield
                b = bank()
                for j in range(TPB):
                    t_v = mm(psum[:, b, j * NG2:(j + 1) * NG2], sq[:, j * P:(j + 1) * P], blk_mean[:], True, True,
                             t_sq, bank_free[b], mark=(j == TPB - 1))
                free["ui"] = t_v
                t_e = dve.add(lambda e: e.tensor_scalar(svar[:], psum[:, b, 0:TPB * NG2], LN_EPS, None, ALU.add), t_v,
                              free.get("svar"))
                bank_free[b] = t_e
                t_r = pool.add(lambda e: e.tensor_tensor(srstd[:], svar[:], mneg_half[:, 0:TPB * NG2], ALU.pow),
                               t_e, free.get("srstd"))
                free["svar"] = t_r
                yield
                t_x = dve.add(lambda e: e.tensor_copy(
                    rexp[:].rearrange("p (j d) -> p j d", d=DIM),
                    srstd[:].rearrange("p (j o) -> p j o", o=1).broadcast_to([P, TPB * NG2, DIM])), t_r, free.get("ur"))
                free["srstd"] = t_x
                b = bank()
                for j in range(TPB):
                    t_t = pe.add(lambda e, j=j: e.transpose(psum[:, b, j * P:(j + 1) * P], rexp[:, j * P:(j + 1) * P],
                                                            ident[:]), t_x, bank_free[b], mark=(j == TPB - 1))
                free["ur"] = t_t
                t_y = dve.add(lambda e: e.tensor_tensor(yn[:], cen[:], psum[:, b, :], ALU.mult), t_t, free.get("zr"))
                free["cen"] = t_y
                bank_free[b] = t_y
                return t_y

            for l in range(DEPTH):
                t_y = yield from norm(t_h)
                t_a = act.add(lambda e: e.activation(act_y[:], yn[:], ACT.Silu, bias=col("ln1_b", l),
                                                     scale=col("ln1_w", l)), t_y, free.get("act_y"))
                free["zr"] = t_a
                yield
                def per_batch(buf):
                    return buf[:].rearrange("p (b t) -> p b t", t=SEQ)
                cw = cosT[:, l:l + 1, :].broadcast_to([P, SW // SEQ, SEQ])
                sw = sinT[:, l:l + 1, :].broadcast_to([P, SW // SEQ, SEQ])
                t_ui = pool.add(lambda e: e.tensor_tensor(per_batch(ui), per_batch(act_y), sw, ALU.mult), t_a, t_tables,
                                free.get("ui"))
                t_ur = dve.add(lambda e: e.tensor_tensor(per_batch(ur), per_batch(act_y), cw, ALU.mult), t_a, t_tables,
                               free.get("ur"))
                free["act_y"] = [t_ui, t_ur]
                rho = sm[:, cols["rho"], l:l + 1].broadcast_to([P, SEQ])

                def scan(dst, src, init, *w):
                    for b in range(SW // SEQ):
                        c_ = slice(b * SEQ, (b + 1) * SEQ)
                        t = dve.add(lambda e, c_=c_: e.tensor_tensor_scan(dst[:, c_], rho, src[:, c_], init,
                                                                          ALU.mult, ALU.add), *w)
                    return t
                t_zr = scan(zr, ur, sm[:, cols["za"], l:l + 1], t_ur, t_state, free.get("zr"))
                yield
                t_zi = scan(zi, ui, sm[:, cols["zb"], l:l + 1], t_ui, t_state, free.get("zi"))
                t_pr = dve.add(lambda e: e.tensor_tensor(per_batch(ur), per_batch(zr), cw, ALU.mult), t_zr)
                t_pi = pool.add(lambda e: e.tensor_tensor(per_batch(ui), per_batch(zi), sw, ALU.mult), t_zi)
                free["zr"], free["zi"] = t_pr, t_pi
                yield
                t_s = dve.add(lambda e: e.tensor_tensor(ur[:], ur[:], ui[:], ALU.add), t_pr, t_pi)
                free["ui"] = t_s
                t_h = dve.add(lambda e: e.scalar_tensor_tensor(out=hh[:], in0=ur[:], scalar=col("sc_lin", l), in1=hh[:],
                                                               op0=ALU.mult, op1=ALU.add), t_s)
                free["ur"] = t_h
                yield
                t_y = yield from norm(t_h)
                t_y2 = dve.add(lambda e: e.tensor_scalar(act_y[:], yn[:], col("ln2_w", l), col("ln2_b", l),
                                                         ALU.mult, ALU.add), t_y, free.get("act_y"))
                free["zr"] = t_y2
                t_sl = []
                for n in range(NG2 * (DFF // P)):
                    g, c = divmod(n, DFF // P)
                    rows = slice(g * DIM, (g + 1) * DIM)
                    b = bank()
                    t_m = mm(psum[:, b, :], w1_sb[rows, l, c * P:(c + 1) * P], act_y[rows, :], True, True, t_y2,
                             t_small, bank_free[b], mark=True)
                    t_s = act.add(lambda e, b=b, n=n, c=c: e.activation(sl[:, n, :], psum[:, b, :], ACT.Silu,
                                                                        bias=b1_sb[:, l, c:c + 1]), t_m, free.get("sl"))
                    bank_free[b] = t_s
                    t_sl.append(t_s)
                    if n % 2:
                        yield
                free["act_y"] = t_m
                b = bank()
                for n in range(NG2 * (DFF // P)):
                    g, c = divmod(n, DFF // P)
                    off = DIM * (NG2 - 1 - g)
                    t_m = mm(psum[:, b, :], w2_sb[:, l * (DFF // P) + c, off:off + P], sl[:, n, :], n == 0,
                             n == NG2 * (DFF // P) - 1, t_sl[n], bank_free[b], mark=True)
                free["sl"] = t_m
                t_h = dve.add(lambda e, b=b: e.scalar_tensor_tensor(out=hh[:], in0=psum[:, b, :], scalar=col("b2", l),
                                                                    in1=hh[:], op0=ALU.add, op1=ALU.add), t_m)
                bank_free[b] = t_h
                yield
            t_y = yield from norm(t_h)
            t_y2 = dve.add(lambda e: e.tensor_scalar(act_y[:], yn[:], col("lnl_w"), col("lnl_b"), ALU.mult, ALU.add),
                           t_y, free.get("act_y"))
            free["zr"] = t_y2
            for n, t in enumerate(tiles):
                g, j = divmod(n, TPB)
                rows = slice(g * DIM, (g + 1) * DIM)
                b = bank()
                t_m = mm(psum[:, b, :], act_y[rows, j * P:(j + 1) * P], wout_sb[rows, :], True, True, t_y2,
                         bank_free[b], mark=True)
                x_ready[t] = dve.add(lambda e, t=t, b=b: e.tensor_tensor(x[:, t, :], x[:, t, :], psum[:, b, :], ALU.add),
                                     t_m, x_ready[t])
                bank_free[b] = x_ready[t]
                if n % 2:
                    yield
            free["act_y"] = t_m

        GATE, UP, AUX = 4, 5, (6, 7)
        weff_slot = [Slot(sem(f"weff_out{i}")) for i in range(2)]
        weff_saved = [None] * IC

        def ffn(F, make_weff, prep, *buffers_free):
            nseq = NBLK * IC
            wgu_free, wdn_free, raw_free = [None] * 2, [None] * 3, [list(buffers_free)] * 2
            gate_free, dT_free, weff_free = [list(buffers_free)] * 2, [None, None], [None]
            d_free = [None]
            aux_turn = [0]

            def fetch(n):
                T, i = divmod(n, IC)
                src = ffn_w[i] if make_weff and T == 0 else weff_dram[i]
                return F["raw_slot"][n % 2].dma(sp, F["raw"][:, n % 2, :], src, raw_free[n % 2],
                                                None if make_weff and T == 0 else weff_saved[i])

            def weights(n, t_raw):
                T, i = divmod(n, IC)
                raw, s, sd = F["raw"][:, n % 2, :], n % 2, n % 3

                def split_both(src, *w):
                    t = split(src[:, 0:2 * DM], F["wgu"][s][0][:], F["wgu"][s][1][:], *w, wgu_free[s])
                    return [t, split(src[:, 2 * DM:], F["wdn"][sd][0][:], F["wdn"][sd][1][:], *w, wdn_free[sd])]
                if not (make_weff and T == 0):
                    raw_free[s] = split_both(raw, t_raw)
                    return raw_free[s]
                cols_ = slice(i * P, (i + 1) * P)
                for kind in range(3):
                    b = AUX[aux_turn[0] % 2]
                    aux_turn[0] += 1
                    if kind < 2:
                        for k in range(KC):
                            t_m = mm(psum[:, b, k * P:(k + 1) * P], short_st[0:96, kind, k * P:(k + 1) * P],
                                     long_st[0:96, cols_], True, True, t_lowrank, bank_free[b], mark=(k == KC - 1))
                    else:
                        t_m = mm(psum[:, b, :], long_st[0:96, cols_], short_st[0:96, kind, :], True, True, t_lowrank,
                                 bank_free[b], mark=True)
                    part = slice(kind * DM, (kind + 1) * DM)
                    t_w = dve.add(lambda e, b=b, part=part: e.tensor_tensor(weff[:, part], raw[:, part], psum[:, b, :],
                                                                            ALU.mult), t_m, t_raw, weff_free[0])
                    bank_free[b] = t_w
                raw_free[s] = t_w
                t = split_both(weff[:], t_w)
                weff_saved[i] = weff_slot[i % 2].dma(sp, weff_dram[i], weff[:], t_w, weff_saved[i - 2] if i >= 2 else None)
                weff_free[0] = [t, weff_saved[i]]
                return t

            g = prep(0)
            t_xT = None
            while True:
                try:
                    next(g)
                except StopIteration as stop:
                    t_xT = stop.value
                    break
            t_raw = {n: fetch(n) for n in range(2)}
            t_w = {0: weights(0, t_raw[0])}
            yield
            down = None
            for T in range(NBLK):
                xT = F["xT"][T % 2]
                ahead = prep(T + 1) if T + 1 < NBLK else iter(())
                t_next = None
                for i in range(IC):
                    n = T * IC + i
                    s = n % 2
                    w, wd = F["wgu"][s], F["wdn"][n % 3]
                    if n + 1 < nseq:
                        t_w[n + 1] = weights(n + 1, t_raw[n + 1]) if n + 1 in t_raw else None
                    if n + 2 < nseq:
                        t_raw[n + 2] = fetch(n + 2)
                    for bank_, off in ((GATE, 0), (UP, DM)):
                        pairs = [((w[0][:, off + k * P:off + (k + 1) * P], w[1][:, off + k * P:off + (k + 1) * P]),
                                  (xT[0][:, k, :], xT[1][:, k, :])) for k in range(KC)]
                        t_m = mm3(psum[:, bank_, :], pairs, t_w[n], t_xT, bank_free[bank_])
                        if bank_ == GATE:
                            t_g = act.add(lambda e, s=s: e.activation(F["gate"][:, s, :], psum[:, GATE, :], ACT.Silu),
                                          t_m, gate_free[s])
                            bank_free[GATE] = t_g
                    if i == IC - 1:
                        F["xT_free"][T % 2] = t_m
                    wgu_free[s] = t_m
                    t_d = dve.add(lambda e, s=s: e.tensor_tensor(F["d"][:], F["gate"][:, s, :], psum[:, UP, :], ALU.mult),
                                  t_m, t_g, d_free[0])
                    bank_free[UP] = t_d
                    gate_free[s] = t_d
                    t_ds = split(F["d"][:], F["dT"][s][0][:], F["dT"][s][1][:], t_d, dT_free[s])
                    d_free[0] = t_ds
                    if down:
                        down()

                    def down(T=T, i=i, s=s, t_ds=t_ds, wd=wd, sd=n % 3):
                        for j in range(TPB):
                            c_ = slice(j * P, (j + 1) * P)
                            pairs = [((F["dT"][s][0][:, c_], F["dT"][s][1][:, c_]), (wd[0][:], wd[1][:]))]
                            t_m = mm3(psum[:, j, :], pairs, t_ds, bank_free[j] if i == 0 else None,
                                      start=(i == 0), stop=(i == IC - 1))
                            if i == IC - 1:
                                t = T * TPB + j
                                x_ready[t] = dve.add(lambda e, t=t, j=j: e.tensor_tensor(
                                    x[:, t, :], x[:, t, :], psum[:, j, :], ALU.add), t_m, x_ready[t])
                                bank_free[j] = x_ready[t]
                        wdn_free[sd] = dT_free[s] = t_m
                    if t_next is None:
                        try:
                            next(ahead)
                        except StopIteration as stop:
                            t_next = stop.value
                    yield
                while t_next is None and T + 1 < NBLK:
                    try:
                        next(ahead)
                    except StopIteration as stop:
                        t_next = stop.value
                t_xT = t_next
            down()

        def block_norm(F, T):
            tiles = list(range(T * TPB, (T + 1) * TPB))
            rs = ln_stats(tiles)
            yield
            xT = F["xT"][T % 2]
            for j, t in enumerate(tiles):
                c_ = slice(j * P, (j + 1) * P)
                t_x = ln_apply(t, rs, F["xn"], AUX[j % 2], xT[0][:, :, c_], xT[1][:, :, c_], F["xT_free"][T % 2])
                yield
            return t_x

        second = {"gen": None}

        def finish_stack():
            for _ in second["gen"]:
                pass

        def norm_after_stack(T):
            if T == NBLK // 2:
                finish_stack()
            t = yield from block_norm(F1, T)
            return t

        for _ in stack_half(0, [0, 1, 2, 3, 4, 5, 6, 7]):
            pass
        second["gen"] = stack_half(1, list(AUX))
        for _ in range(2 + TPB + 2 + TPB + 1):
            next(second["gen"], None)
        STRIDE = 6
        for _ in ffn(F1, True, norm_after_stack, t_lowrank, t_tables):
            for _ in range(STRIDE):
                next(second["gen"], None)
        finish_stack()
        barrier()
        phase1.close()

        phase2 = ExitStack()

        def sb2(name, shape, dt=F32):
            return sb(name, shape, dt, phase2)
        axT = [sb2(f"axT_{p}", [P, KC, TOK], F32R) for p in "hl"]
        KVQ = 2 * HD + GRP * HD
        stage = sb2("stage", [P, KC * KVQ])
        wkvq = [sb2(f"wkvq_{p}", [P, KC, KVQ], F32R) for p in "hl"]
        wo_s = [sb2(f"wo_{p}", [P, GRP, DM], F32R) for p in "hl"]
        qT = [sb2(f"qT_{p}", [P, GRP, SEQ], F32R) for p in "hl"]
        kT = [sb2(f"kT_{p}", [P, SEQ], F32R) for p in "hl"]
        vv = [[sb2(f"v{s}_{p}", [P, STILES, HD], F32R) for p in "hl"] for s in range(2)]
        oT = [sb2(f"oT_{p}", [P, GRP, SEQ], F32R) for p in "hl"]
        q_tok = sb2("q_tok", [P, STILES, GRP * HD])
        k_tok = sb2("k_tok", [P, STILES, HD])
        squares = sb2("squares", [P, GRP * HD])
        SC = P + SEQ
        biased = sb2("biased", [P, 2, SC])
        prob = sb2("prob", [P, GRP, SC])
        pT = [[sb2(f"pT{s}_{p}", [P, SC], F32R) for p in "hl"] for s in range(2)]
        alibi = sb2("alibi", [P, GRP, SC])
        rel = sb2("rel", [P, SC])
        future = sb2("future", [P, SC])
        qkw = sb2("qkw", [P, 2, HD])
        kw = sb2("kw", [P, HD])
        ss_q = sb2("ss_q", [P, STILES, GRP])
        r_q = sb2("r_q", [P, STILES, GRP])
        ss_k = sb2("ss_k", [P, STILES])
        r_k = sb2("r_k", [P, STILES])
        nmax = sb2("nmax", [P, GRP, STILES])
        esum = sb2("esum", [P, GRP, STILES])
        rsum = sb2("rsum", [P, GRP, STILES])
        KV, QB, WO = 4, (5, 6), 7

        slot_stage = Slot(sem("stage_in"))
        stage_free = [None]
        t_qkw = Slot(sem("qkw_in")).dma(sp, qkw[:], qk_w.partition_broadcast(P))
        t_kw = dve.add(lambda e: e.tensor_tensor(kw[:], qkw[:, 0, :], qkw[:, 1, :], ALU.mult), t_qkw)
        pool.add(lambda e: e.iota(rel[:, 0:P], [[1, P]], base=0, channel_multiplier=-1,
                                  allow_small_or_imprecise_dtypes=True))
        t_rel = pool.add(lambda e: e.iota(rel[:, P:], [[1, SEQ]], base=-P, channel_multiplier=-1,
                                          allow_small_or_imprecise_dtypes=True))
        t_fut = dve.add(lambda e: e.tensor_scalar(future[:], rel[:], 0.0, NEG_INF, ALU.is_gt, ALU.mult), t_rel)

        t_wkvq, wkvq_free = [None], [None]
        t_wo, wo_free = [None], [None]

        def load_kvq(g):
            return slot_stage.dma(sp, stage[:], wqkv[g], stage_free[0])

        def split_kvq(t):
            t_wkvq[0] = split(stage[:].rearrange("p (k n) -> p k n", k=KC), wkvq[0][:], wkvq[1][:], t, wkvq_free[0])
            stage_free[0] = t_wkvq[0]

        def load_wo(g):
            return slot_stage.dma(sp, stage[:, 0:GRP * DM], wo[g], stage_free[0])

        def split_wo(t):
            t_wo[0] = split(stage[:, 0:GRP * DM].rearrange("p (h n) -> p h n", h=GRP), wo_s[0][:], wo_s[1][:], t,
                            wo_free[0])
            stage_free[0] = t_wo[0]

        split_kvq(load_kvq(0))
        t_wo_load = load_wo(0)

        rs = [ln_stats(list(range(T * TPB, (T + 1) * TPB))) for T in range(NBLK)]
        t_ax = [None] * NT
        xn_users[:] = [None, None]

        def norm_tile(t):
            c_ = slice(t * P, (t + 1) * P)
            t_ax[t] = ln_apply(t, rs[t // TPB], q_tok, QB[t % 2], axT[0][:, :, c_], axT[1][:, :, c_])

        for t in range(NT):
            norm_tile(t)

        t_al, al_free = [None], [None]

        def alibi_tables(g):
            for hd in range(GRP):
                t_al[0] = dve.add(lambda e, hd=hd: e.scalar_tensor_tensor(
                    out=alibi[:, hd, :], in0=rel[:], scalar=SLOPES[g * GRP + hd], in1=future[:],
                    op0=ALU.mult, op1=ALU.add), t_fut, al_free[0])

        ft = {"v": [None, None], "kT": None, "qT": None, "k_tok": None, "q_tok": [None, None], "oT": None,
              "biased": [None, None], "prob": [None] * GRP, "pT": [None, None], "sq": None}
        tk = {}

        def kv_proj(u):
            g, b = divmod(u, BATCH)
            s = u % 2
            for t in range(STILES):
                tile = b * STILES + t
                c_ = slice(tile * P, (tile + 1) * P)
                pairs = [((axT[0][:, k, c_], axT[1][:, k, c_]), (wkvq[0][:, k, 0:2 * HD], wkvq[1][:, k, 0:2 * HD]))
                         for k in range(KC)]
                t_m = mm3(psum[:, KV, t * 2 * HD:(t + 1) * 2 * HD], pairs, t_ax[tile], t_wkvq[0], bank_free[KV])
            kv = psum[:, KV, :].rearrange("p (t n) -> p t n", t=STILES)
            for t in range(STILES):
                t_ss = act.add(lambda e, t=t: e.activation(squares[:, t * HD:(t + 1) * HD], kv[:, t, 0:HD], ACT.Square,
                                                           accum_out=ss_k[:, t:t + 1]), t_m, ft["sq"], ft["k_tok"])
            ft["sq"] = t_ss
            t_a = pool.add(lambda e: e.tensor_scalar(ss_k[:], ss_k[:], 1.0 / HD, RMS_EPS, ALU.mult, ALU.add), t_ss)
            t_r = pool.add(lambda e: e.tensor_tensor(r_k[:], ss_k[:], mneg_half[:, 0:STILES], ALU.pow), t_a)
            t_v = split(kv[:, :, HD:2 * HD], vv[s][0][:], vv[s][1][:], t_m, ft["v"][s])
            for t in range(STILES):
                t_k = dve.add(lambda e, t=t: e.scalar_tensor_tensor(out=k_tok[:, t, :], in0=kv[:, t, 0:HD],
                                                                    scalar=r_k[:, t:t + 1], in1=kw[:], op0=ALU.mult,
                                                                    op1=ALU.mult), t_r, t_kw, ft["k_tok"])
            bank_free[KV] = [t_v, t_k]
            tk["v"], tk["k"] = t_v, t_k

        def k_transpose(u):
            for t in range(STILES):
                t_t = pe.add(lambda e, t=t: e.transpose(psum[:, KV, t * P:(t + 1) * P], k_tok[:, t, :], ident[:]),
                             tk["k"], bank_free[KV], mark=(t == STILES - 1))
            ft["k_tok"] = t_t
            tk["kT"] = bank_free[KV] = split(psum[:, KV, 0:SEQ], kT[0][:], kT[1][:], t_t, ft["kT"])

        def q_proj(u, t):
            g, b = divmod(u, BATCH)
            tile = b * STILES + t
            c_ = slice(tile * P, (tile + 1) * P)
            pairs = [((axT[0][:, k, c_], axT[1][:, k, c_]), (wkvq[0][:, k, 2 * HD:], wkvq[1][:, k, 2 * HD:]))
                     for k in range(KC)]
            t_m = mm3(psum[:, QB[t], :], pairs, t_ax[tile], t_wkvq[0], bank_free[QB[t]])
            if t == STILES - 1 and b == BATCH - 1:
                wkvq_free[0] = t_m
            t_sq = act.add(lambda e: e.activation(squares[:], psum[:, QB[t], :], ACT.Square), t_m, ft["sq"])
            t_ss = dve.add(lambda e: e.tensor_reduce(ss_q[:, t, :], squares[:].rearrange("p (h d) -> p h d", h=GRP),
                                                     AX.X, ALU.add), t_sq, ft["q_tok"][t])
            ft["sq"] = t_ss
            t_a = pool.add(lambda e: e.tensor_scalar(ss_q[:, t, :], ss_q[:, t, :], 1.0, HD * RMS_EPS, ALU.mult, ALU.add),
                           t_ss)
            t_r = pool.add(lambda e: e.tensor_tensor(r_q[:, t, :], ss_q[:, t, :], mneg_half[:, 0:GRP], ALU.pow), t_a)
            tk["qr", t] = t_r

        def q_scale(u, t):
            t_q = dve.add(lambda e: e.tensor_tensor(
                q_tok[:, t, :].rearrange("p (h d) -> p h d", h=GRP),
                psum[:, QB[t], :].rearrange("p (h d) -> p h d", h=GRP),
                r_q[:, t, :].rearrange("p (h o) -> p h o", o=1).broadcast_to([P, GRP, HD]), ALU.mult),
                tk["qr", t], ft["q_tok"][t])
            bank_free[QB[t]] = t_q
            tk["q", t] = t_q

        def q_transpose(u, t):
            for hd in range(GRP):
                t_t = pe.add(lambda e, hd=hd: e.transpose(psum[:, QB[t], hd * P:(hd + 1) * P],
                                                          q_tok[:, t, hd * HD:(hd + 1) * HD], ident[:]),
                             tk["q", t], bank_free[QB[t]], mark=(hd == GRP - 1))
            ft["q_tok"][t] = t_t
            c_ = slice(t * P, (t + 1) * P)
            tk["qT", t] = bank_free[QB[t]] = split(psum[:, QB[t], :].rearrange("p (h c) -> p h c", h=GRP),
                                                   qT[0][:, :, c_], qT[1][:, :, c_], t_t, ft["qT"])

        def scores(u, hd):
            s = hd % 2
            part = ((0, P), (P, SC))
            for t in range(STILES):
                a, b_ = part[t]
                q_ = slice(t * P, (t + 1) * P)
                pairs = [((qT[0][:, hd, q_], qT[1][:, hd, q_]), (kT[0][:, 0:b_ - a], kT[1][:, 0:b_ - a]))]
                t_m = mm3(psum[:, hd, a:b_], pairs, tk["qT", t], tk["kT"], bank_free[hd])
            ft["qT"] = ft["kT"] = t_m
            for t in range(STILES):
                a, b_ = part[t]
                t_b = dve.add(lambda e, t=t, a=a, b_=b_: e.tensor_tensor_reduce(
                    biased[:, s, a:b_], psum[:, hd, a:b_], alibi[:, hd, a:b_], -1.0, 3e38, ALU.add, ALU.min,
                    nmax[:, hd, t:t + 1]), t_m, t_al[0], ft["biased"][s])
                t_e = act.add(lambda e, t=t, a=a, b_=b_: e.activation(
                    prob[:, hd, a:b_], biased[:, s, a:b_], ACT.Exp, bias=nmax[:, hd, t:t + 1], scale=-1.0,
                    accum_out=esum[:, hd, t:t + 1]), t_b, ft["prob"][hd])
            bank_free[hd] = al_free[0] = t_b
            ft["biased"][s] = t_e
            t_r = dve.add(lambda e: e.reciprocal(rsum[:, hd, :], esum[:, hd, :]), t_e)
            for t in range(STILES):
                a, b_ = part[t]
                t_p = pool.add(lambda e, t=t, a=a, b_=b_: e.tensor_scalar(prob[:, hd, a:b_], prob[:, hd, a:b_],
                                                                          rsum[:, hd, t:t + 1], 1.0, ALU.mult, ALU.mult), t_r)
            tk["p", hd] = t_p

        def p_transpose(u, hd):
            s = hd % 2
            for n in range(SC // P):
                t_t = pe.add(lambda e, n=n: e.transpose(psum[:, hd, n * P:(n + 1) * P], prob[:, hd, n * P:(n + 1) * P],
                                                        ident[:]), tk["p", hd], bank_free[hd], mark=(n == SC // P - 1))
            ft["prob"][hd] = t_t
            tk["pT", hd] = bank_free[hd] = split(psum[:, hd, 0:SC], pT[s][0][:], pT[s][1][:], t_t, ft["pT"][s])

        def attend(u, hd):
            s, v = hd % 2, vv[u % 2]
            mm3(psum[:, hd, 0:SEQ], [((v[0][:, 0, :], v[1][:, 0, :]), (pT[s][0][:, 0:SEQ], pT[s][1][:, 0:SEQ]))],
                tk["pT", hd], tv[u % 2], bank_free[hd], stop=False)
            t_m = mm3(psum[:, hd, P:SEQ], [((v[0][:, 1, :], v[1][:, 1, :]), (pT[s][0][:, SEQ:], pT[s][1][:, SEQ:]))],
                      start=False)
            ft["pT"][s] = t_m
            ft["v"][u % 2] = t_m
            tk["oT", hd] = bank_free[hd] = split(psum[:, hd, 0:SEQ], oT[0][:, hd, :], oT[1][:, hd, :], t_m, ft["oT"])

        def out_proj(u, t):
            g, b = divmod(u, BATCH)
            tile = b * STILES + t
            c_ = slice(t * P, (t + 1) * P)
            pe.wait(bank_free[WO], t_wo[0])
            for hd in range(GRP):
                t_m = mm3(psum[:, WO, :], [((oT[0][:, hd, c_], oT[1][:, hd, c_]), (wo_s[0][:, hd, :], wo_s[1][:, hd, :]))],
                          tk["oT", hd], start=(hd == 0), stop=(hd == GRP - 1))
            if t == STILES - 1:
                ft["oT"] = t_m
                if b == BATCH - 1:
                    wo_free[0] = t_m
            x_ready[tile] = dve.add(lambda e: e.tensor_tensor(x[:, tile, :], x[:, tile, :], psum[:, WO, :], ALU.add),
                                    t_m, x_ready[tile])
            bank_free[WO] = x_ready[tile]

        tv = [None, None]
        units = KVH * BATCH
        alibi_tables(0)
        split_wo(t_wo_load)
        kv_proj(0)
        tv[0] = tk["v"]
        for t in range(STILES):
            q_proj(0, t)
            q_scale(0, t)
        k_transpose(0)
        for t in range(STILES):
            q_transpose(0, t)
        t_next_kvq = load_kvq(1)
        t_next_wo = None
        for u in range(units):
            g, b = divmod(u, BATCH)
            nxt = u + 1 < units
            if b == 0 and g > 0:
                alibi_tables(g)
                split_wo(t_next_wo)
                if g + 1 < KVH:
                    t_next_kvq = load_kvq(g + 1)
            for hd in range(GRP):
                scores(u, hd)
            if nxt:
                kv_proj(u + 1)
                tv[(u + 1) % 2] = tk["v"]
            p_transpose(u, 0)
            p_transpose(u, 1)
            if nxt:
                q_proj(u + 1, 0)
            attend(u, 0)
            attend(u, 1)
            if nxt:
                q_scale(u + 1, 0)
            p_transpose(u, 2)
            p_transpose(u, 3)
            if nxt:
                q_proj(u + 1, 1)
            attend(u, 2)
            attend(u, 3)
            if nxt:
                q_scale(u + 1, 1)
                k_transpose(u + 1)
                q_transpose(u + 1, 0)
            if b == BATCH - 2 and g + 1 < KVH:
                split_kvq(t_next_kvq)
                t_next_wo = load_wo(g + 1)
            out_proj(u, 0)
            if nxt:
                q_transpose(u + 1, 1)
            out_proj(u, 1)
        barrier()
        phase2.close()

        phase3 = ExitStack()
        F2 = ffn_buffers(phase3, "b")
        xn_users[:] = [None, None]
        for _ in ffn(F2, False, lambda T: block_norm(F2, T)):
            pass
        ov = out.rearrange("(t p) d -> p t d", p=P)
        for c in range(NBLK):
            t_out = Slot(sem(f"x_out{c}")).dma(sp, ov[:, c * TPB:(c + 1) * TPB, :], x[:, c * TPB:(c + 1) * TPB, :],
                                               x_ready[(c + 1) * TPB - 1])
            sp.wait(t_out)
        phase3.close()


def kernel(**inputs):
    import concourse.bacc as bacc
    from concourse.bass_utils import run_bass_kernel_spmd

    a = {n[3:]: np.asarray(v) for n, v in inputs.items()}
    x = a["attn_a_x"].reshape(TOK, DM)
    win = a["attn_a_Win"].T
    vecs = np.concatenate([a["attn_a_" + n].T.reshape(DIM, w) for n, (_, w) in VEC.items()], axis=1)
    b1 = a["attn_a_b1"].reshape(DEPTH, DFF // P, P).transpose(2, 0, 1)
    w1 = a["attn_a_W1"].transpose(2, 0, 1)
    w2 = a["attn_a_W2"].transpose(0, 2, 1).reshape(DEPTH, DFF // P, P, DIM).transpose(2, 0, 1, 3).reshape(P, -1, DIM)
    wout = a["attn_a_Wout"].T

    def in_out(w):
        return w.reshape(IC, P, KC, P).transpose(0, 3, 2, 1).reshape(IC, P, DM)
    ffn_w = np.concatenate([in_out(a["ffn_gate_w"]), in_out(a["ffn_up_w"]),
                            a["ffn_down_w"].T.reshape(IC, P, DM)], axis=2)
    lr_long = np.concatenate([a["ffn_gate_su"].T, a["ffn_up_su"].T, a["ffn_down_sv"]], axis=0)
    lr_short = np.concatenate([a["ffn_gate_sv"], a["ffn_up_sv"], a["ffn_down_su"].T], axis=0)

    def by_group(w, n):
        return w.reshape(KVH, n, KC, P).transpose(0, 3, 2, 1)
    wqkv = np.concatenate([by_group(a["attn_b_Wk"], HD), by_group(a["attn_b_Wv"], HD),
                           by_group(a["attn_b_Wq"], GRP * HD)], axis=3).reshape(KVH, P, -1)
    wo = a["attn_b_Wo"].reshape(DM, KVH, GRP, HD).transpose(1, 3, 2, 0).reshape(KVH, HD, -1)
    qk_w = np.stack([a["attn_b_q_norm_w"], a["attn_b_k_norm_w"]])

    nc = bacc.Bacc("TRN2", target_bir_lowering=False, num_devices=1)
    arrays, args = {}, []
    for name, v in (("x", x), ("win", win), ("vecs", vecs), ("b1", b1), ("w1", w1), ("w2", w2), ("wout", wout),
                    ("bout", a["attn_a_bout"]), ("ffn_w", ffn_w), ("lr_long", lr_long), ("lr_short", lr_short),
                    ("wqkv", wqkv), ("wo", wo), ("qk_w", qk_w)):
        name = "in_" + name
        arrays[name] = np.ascontiguousarray(v)
        args.append(nc.dram_tensor(name, arrays[name].shape, F32, kind="ExternalInput").ap())
    args.append(nc.dram_tensor("out", (TOK, DM), F32, kind="ExternalOutput").ap())
    args.append(nc.dram_tensor("weff_dram", (IC, P, 3 * DM), F32, kind="Internal").ap())
    hybrid_block(nc, *args)
    r = run_bass_kernel_spmd(nc, [arrays], core_ids=[0])
    return r.results[0]["out"].reshape(BATCH, SEQ, DM)
```

```python
from contextlib import ExitStack
import math

import numpy as np

import concourse.bass as bass
from concourse import mybir

F32 = mybir.dt.float32
F32R = mybir.dt.float32r
ALU = mybir.AluOpType
ACT = mybir.ActivationFunctionType
AX = mybir.AxisListType

P = 128
BATCH, SEQ, DM = 8, 256, 512
TOK = BATCH * SEQ
NT = TOK // P
KC = DM // P
BLK = 512
TPB = BLK // P
NBLK = TOK // BLK
DEPTH, DIM, DFF = 4, 64, 256
NG2 = P // DIM
INNER, RANK = 1792, 4
IC = INNER // P
HEADS, KVH, HD = 32, 8, 128
GRP = HEADS // KVH
STILES = SEQ // P
LN_EPS, RMS_EPS = 1e-5, 1e-6
NEG_INF = -1e30
SLOPE0 = 2 ** (-2 ** (-(math.log2(HEADS) - 3)))
SLOPES = [float(np.float32(SLOPE0 * SLOPE0 ** i)) for i in range(HEADS)]

VEC = {}
for _n, _w in (("ln1_w", DEPTH), ("ln1_b", DEPTH), ("phz_re", DEPTH), ("phz_im", DEPTH), ("lc_re", DEPTH),
               ("lc_im", DEPTH), ("sc_lin", DEPTH), ("ln2_w", DEPTH), ("ln2_b", DEPTH), ("b2", DEPTH),
               ("bin", 1), ("lnl_w", 1), ("lnl_b", 1)):
    VEC[_n] = (sum(w for _, w in VEC.values()), _w)
NVEC = sum(w for _, w in VEC.values())

PASSES = ((0, 0), (0, 1), (1, 0))


class Lane:

    def __init__(self, engine, sem):
        self.engine, self.sem, self.count, self.seen = engine, sem, 0, {}

    def wait(self, *tickets):
        for t in tickets:
            if t is None:
                continue
            if isinstance(t, list):
                self.wait(*t)
                continue
            sem, value = t
            if self.seen.get(id(sem), 0) < value:
                self.seen[id(sem)] = value
                self.engine.wait_ge(sem, value)

    def add(self, fn, *waits, mark=True):
        self.wait(*waits)
        ins = fn(self.engine)
        if not mark:
            return None
        ins.then_inc(self.sem, 1)
        self.count += 1
        return (self.sem, self.count)

    def now(self):
        return (self.sem, self.count) if self.count else None


class Slot:

    def __init__(self, sem):
        self.sem, self.count = sem, 0

    def dma(self, lane, dst, src, *waits):
        lane.wait(*waits)
        self.count += 16
        lane.engine.dma_start(dst, src).then_inc(self.sem, 16)
        return (self.sem, self.count)


def hybrid_block(nc, x_in, win, vecs, b1, w1, w2, wout, bout, ffn_w, lr_long, lr_short, wqkv, wo, qk_w, out, weff_dram):
    with ExitStack() as ctx:
        def sb(name, shape, dt=F32, stack=None):
            return (stack or ctx).enter_context(nc.sbuf_tensor(name, shape, dt))

        def sem(name):
            return ctx.enter_context(nc.semaphore(name))

        pe, act, dve, pool, sp = (Lane(engine, sem(name)) for engine, name in (
            (nc.tensor, "pe_done"), (nc.scalar, "act_done"), (nc.vector, "dve_done"), (nc.gpsimd, "pool_done"),
            (nc.sync, "sp_done")))
        psum = ctx.enter_context(nc.psum_tensor("psum", [P, 8, 512], F32))
        bank_free = [None] * 8

        x = sb("x", [P, NT, DM])
        ident = sb("ident", [P, P])
        mneg_half = sb("mneg_half", [P, 16])
        ln_mv = sb("ln_mv", [P, NT, 2])
        ln_bn = sb("ln_bn", [P, 2, 6])
        ln_var = sb("ln_var", [P, NT])
        ln_rstd = sb("ln_rstd", [P, NT])
        x_ready = [None] * NT
        stage = sb("stage", [P, 2, 3 * DM])
        stage_slot = [Slot(sem(f"stage{i}")) for i in range(2)]
        stage_free = [None, None]

        def split(src, hi, lo, *ready, on=None):
            t_hi = act.add(lambda e: e.activation(hi, src, ACT.Copy), *ready)
            t_lo = (on or dve).add(lambda e: e.tensor_tensor(lo, src, hi.bitcast(F32), ALU.subtract), t_hi, *ready)
            return t_lo

        def mm(out_ap, lhsT, rhs, start, stop, *waits, mark=False):
            return pe.add(lambda e: e.matmul(out_ap, lhsT, rhs, start=start, stop=stop), *waits, mark=mark)

        def mm3(out_ap, pairs, *waits, start=True, stop=True):
            pe.wait(*waits)
            n, last = 0, len(pairs) * len(PASSES) - 1
            for stat, mov in pairs:
                for a, b in PASSES:
                    t = mm(out_ap, stat[a], mov[b], start and n == 0, stop and n == last, mark=(n == last))
                    n += 1
            return t

        t_id0 = pool.add(lambda e: e.memset(ident[:], 0.0))
        t_ident = pool.add(lambda e: e.affine_select(out=ident[:], in_=ident[:], compare_op=ALU.not_equal, fill=1.0,
                                                     base=0, pattern=[[-1, P]], channel_multiplier=1), t_id0)
        t_half = pool.add(lambda e: e.memset(mneg_half[:], -0.5))

        def ln_stats(tiles):
            a, b = tiles[0], tiles[-1] + 1
            for t in tiles:
                t_bn = dve.add(lambda e, t=t: e.bn_stats(ln_bn[:, t % 2, :], x[:, t, :]), x_ready[t])
                t_mv = dve.add(lambda e, t=t: e.bn_aggr(ln_mv[:, t, :], ln_bn[:, t % 2, :]), t_bn)
            t_v = pool.add(lambda e: e.tensor_scalar(ln_var[:, a:b], ln_mv[:, a:b, 1], LN_EPS, None, ALU.add), t_mv)
            return pool.add(lambda e: e.tensor_tensor(ln_rstd[:, a:b], ln_var[:, a:b], mneg_half[:, 0:b - a], ALU.pow),
                            t_v, t_half)

        xn_users = [None, None]
        turn = {"xn": 0}

        def ln_apply(t, t_rstd, xn, bank, hi, lo, *dst_free):
            s = turn["xn"] % 2
            turn["xn"] += 1
            t_xn = dve.add(lambda e: e.tensor_scalar(xn[:, s, :], x[:, t, :], ln_mv[:, t, 0:1], ln_rstd[:, t:t + 1],
                                                     ALU.subtract, ALU.mult), t_rstd, xn_users[s])
            for k in range(KC):
                t_tr = pe.add(lambda e, k=k: e.transpose(psum[:, bank, k * P:(k + 1) * P], xn[:, s, k * P:(k + 1) * P],
                                                         ident[:]), t_xn, t_ident, bank_free[bank], mark=(k == KC - 1))
            xn_users[s] = t_tr
            src = psum[:, bank, :].rearrange("p (k c) -> p k c", k=KC)
            bank_free[bank] = split(src, hi, lo, t_tr, *dst_free)
            return bank_free[bank]

        def barrier(*others):
            marks = [l.now() for l in (pe, act, dve, pool)] + list(others)
            for l in (pe, act, dve, pool):
                l.wait(*marks)
            return marks

        phase1 = ExitStack()
        win_raw = sb("win_raw", [P, KC, DIM], F32, phase1)
        win_hi = sb("win_hi", [P, KC, 3 * DIM], F32R, phase1)
        win_lo = sb("win_lo", [P, KC, 3 * DIM], F32R, phase1)
        vec = sb("vec", [P, NVEC], F32, phase1)
        b1_sb = sb("b1_sb", [P, DEPTH, DFF // P], F32, phase1)
        w1_sb = sb("w1_sb", [P, DEPTH, DFF], F32, phase1)
        w2_sb = sb("w2_sb", [P, DEPTH * (DFF // P), 3 * DIM], F32, phase1)
        wout_sb = sb("wout_sb", [P, DM], F32, phase1)
        bout_sb = sb("bout_sb", [P, DM], F32, phase1)
        center = sb("center", [P, P], F32, phase1)
        blk_mean = sb("blk_mean", [P, NG2], F32, phase1)
        cosT = sb("cosT", [P, DEPTH, SEQ], F32, phase1)
        sinT = sb("sinT", [P, DEPTH, SEQ], F32, phase1)
        sm = sb("sm", [P, 32, DEPTH], F32, phase1)
        STEPS_APART = 7
        NS = NBLK
        SW = BLK // NG2
        SJ = SW // P
        h = [sb(f"h{i}", [P, SW], F32, phase1) for i in range(NS)]
        buf_a, buf_b, buf_c, buf_d, buf_e = ([sb(f"buf_{n}{i}", [P, SW], F32, phase1) for i in range(NS)] for n in "abcde")
        sl = sb("sl", [P, 2, DFF // P, NG2 * SW], F32, phase1)
        svar = sb("svar", [P, NS, SJ * NG2], F32, phase1)
        srstd = sb("srstd", [P, NS, SJ * NG2], F32, phase1)

        def ffn_buffers(stack, tag):
            d = {}
            d["xn"] = sb(f"xn{tag}", [P, 2, DM], F32, stack)
            d["xT"] = [[sb(f"xT{s}{part}{tag}", [P, KC, BLK], F32R, stack) for part in "hl"] for s in range(2)]
            d["wgu"] = [[sb(f"wgu{s}{part}{tag}", [P, 2 * DM], F32R, stack) for part in "hl"] for s in range(2)]
            d["wdn"] = [[sb(f"wdn{s}{part}{tag}", [P, DM], F32R, stack) for part in "hl"] for s in range(3)]
            d["gate"] = sb(f"gate{tag}", [P, 2, BLK], F32, stack)
            d["d"] = sb(f"d{tag}", [P, BLK], F32, stack)
            d["dT"] = [[sb(f"dT{s}{part}{tag}", [P, BLK], F32R, stack) for part in "hl"] for s in range(2)]
            d["xT_free"] = [None, None]
            return d

        F1 = ffn_buffers(phase1, "a")
        weff = sb("weff", [P, 3 * DM], F32, phase1)
        LR_ROWS = 3 * RANK
        long_raw = sl[:].rearrange("p s n c -> p (s n c)")[:, 0:INNER]
        short_raw = stage[:, 1, :].rearrange("p (n d) -> p n d", n=3)
        tab = F1["gate"][:, 0, :].rearrange("p (l t) -> p l t", l=DEPTH)
        tab2 = F1["gate"][:, 1, :].rearrange("p (l t) -> p l t", l=DEPTH)
        long_st = sb("long_st", [P, INNER], F32R, phase1)
        short_st = sb("short_st", [P, 3, DM], F32R, phase1)

        s_vec = Slot(sem("vec_in"))
        for g in range(NG2):
            t_vec = s_vec.dma(sp, vec[g * DIM:(g + 1) * DIM, :], vecs)
        xv = x_in.rearrange("(t p) d -> p t d", p=P)
        for c in range(NBLK):
            t = Slot(sem(f"x_in{c}")).dma(sp, x[:, c * TPB:(c + 1) * TPB, :], xv[:, c * TPB:(c + 1) * TPB, :])
            for j in range(TPB):
                x_ready[c * TPB + j] = t
        t_zero_w2 = pool.add(lambda e: e.memset(w2_sb[:], 0.0))
        t_zero_long = dve.add(lambda e: e.memset(long_raw, 0.0))
        t_zero_short = dve.add(lambda e: e.memset(short_raw, 0.0))
        t_win = Slot(sem("win_in")).dma(sp, win_raw[:], win.rearrange("(k p) d -> p k d", p=P))
        s_small = Slot(sem("small_in"))
        for g in range(NG2):
            rows = slice(g * DIM, (g + 1) * DIM)
            s_small.dma(sp, w1_sb[rows, :, :], w1)
            s_small.dma(sp, wout_sb[rows, :], wout)
        s_small.dma(sp, b1_sb[:], b1)
        s_small.dma(sp, bout_sb[:], bout.partition_broadcast(P))
        t_small = s_small.dma(sp, w2_sb[:, :, DIM:2 * DIM], w2, t_zero_w2)
        s_lr = Slot(sem("lr_in"))
        for q in range(3):
            s_lr.dma(sp, long_raw[32 * q:32 * q + LR_ROWS, :], lr_long, t_zero_long)
            for kind in range(3):
                r = 32 * q + RANK * kind
                t_lr = s_lr.dma(sp, short_raw[r:r + RANK, kind, :], lr_short[RANK * kind:RANK * (kind + 1), :],
                                t_zero_short)

        t_wz0 = dve.add(lambda e: e.memset(win_hi[:].bitcast(F32), 0.0))
        t_wz1 = dve.add(lambda e: e.memset(win_lo[:].bitcast(F32), 0.0))
        t_winr = split(win_raw[:], win_hi[:, :, DIM:2 * DIM], win_lo[:, :, DIM:2 * DIM], t_win, t_wz0, t_wz1)

        t_c = pool.add(lambda e: e.memset(blk_mean[:], 0.0))
        t_c = pool.add(lambda e: e.memset(center[:], 0.0), t_c)
        for g in range(NG2):
            rows = slice(g * DIM, (g + 1) * DIM)
            pool.add(lambda e, r=rows, g=g: e.memset(blk_mean[r, g:g + 1], 1.0 / DIM), t_c)
            t_c2 = pool.add(lambda e, r=rows: e.memset(center[r, r], -1.0 / DIM), t_c)
        t_center = pool.add(lambda e: e.tensor_tensor(center[:], center[:], ident[:], ALU.add), t_c2, t_ident)

        def col(name, layer=None):
            a, w = VEC[name]
            return vec[:, a:a + w] if layer is None else vec[:, a + layer:a + layer + 1]

        cols = {n: i for i, n in enumerate(("m", "a", "b", "q", "z", "ri", "c1", "s1", "r", "rho", "t0", "t1", "t2",
                                            "mt", "za", "zb", "pc", "ps", "pc2", "ps2", "absi"))}

        def C(n):
            return sm[:, cols[n], :]

        x_read = {}
        rs0 = [ln_stats(list(range(T * TPB, (T + 1) * TPB))) for T in range(NBLK)]
        chain = [dve.add(lambda e: e.memset(sm[:], 0.0))]

        def step(lane, fn):
            chain[0] = lane.add(fn, chain[0])
            return chain[0]

        dve.wait(t_vec)
        step(dve, lambda e: e.tensor_scalar(C("m"), col("phz_re"), -1.0, None, ALU.mult))
        step(dve, lambda e: e.tensor_tensor(C("m"), C("m"), col("phz_re"), ALU.max))
        step(dve, lambda e: e.tensor_scalar(C("absi"), col("phz_im"), -1.0, None, ALU.mult))
        step(dve, lambda e: e.tensor_tensor(C("absi"), C("absi"), col("phz_im"), ALU.max))
        step(dve, lambda e: e.tensor_tensor(C("m"), C("m"), C("absi"), ALU.max))
        step(dve, lambda e: e.tensor_scalar(C("m"), C("m"), 1e-30, None, ALU.max))
        step(dve, lambda e: e.reciprocal(C("t0"), C("m")))
        step(dve, lambda e: e.tensor_tensor(C("a"), col("phz_re"), C("t0"), ALU.mult))
        step(dve, lambda e: e.tensor_tensor(C("b"), col("phz_im"), C("t0"), ALU.mult))
        step(dve, lambda e: e.tensor_tensor(C("q"), C("a"), C("a"), ALU.mult))
        step(dve, lambda e: e.tensor_tensor(C("t1"), C("b"), C("b"), ALU.mult))
        step(dve, lambda e: e.tensor_tensor(C("q"), C("q"), C("t1"), ALU.add))
        step(dve, lambda e: e.tensor_scalar(C("z"), C("q"), 0.0, None, ALU.is_equal))
        step(dve, lambda e: e.tensor_tensor(C("q"), C("q"), C("z"), ALU.add))
        step(dve, lambda e: e.tensor_tensor(C("a"), C("a"), C("z"), ALU.add))
        step(pool, lambda e: e.tensor_tensor(C("ri"), C("q"), mneg_half[:, 0:DEPTH], ALU.pow))
        step(dve, lambda e: e.tensor_tensor(C("t0"), C("ri"), C("ri"), ALU.mult))
        step(dve, lambda e: e.tensor_tensor(C("t0"), C("t0"), C("q"), ALU.mult))
        step(dve, lambda e: e.tensor_scalar(C("t0"), C("t0"), -0.5, 1.5, ALU.mult, ALU.add))
        step(dve, lambda e: e.tensor_tensor(C("ri"), C("ri"), C("t0"), ALU.mult))
        step(dve, lambda e: e.tensor_tensor(C("c1"), C("a"), C("ri"), ALU.mult))
        step(dve, lambda e: e.tensor_tensor(C("s1"), C("b"), C("ri"), ALU.mult))
        step(dve, lambda e: e.tensor_tensor(C("r"), C("q"), C("ri"), ALU.mult))
        step(dve, lambda e: e.tensor_tensor(C("r"), C("r"), C("m"), ALU.mult))
        step(act, lambda e: e.activation(C("rho"), C("r"), ACT.Tanh))
        step(dve, lambda e: e.tensor_tensor(C("t0"), C("c1"), col("lc_re"), ALU.mult))
        step(dve, lambda e: e.tensor_tensor(C("t1"), C("s1"), col("lc_im"), ALU.mult))
        step(dve, lambda e: e.tensor_tensor(C("za"), C("t0"), C("t1"), ALU.subtract))
        step(dve, lambda e: e.tensor_tensor(C("t0"), C("c1"), col("lc_im"), ALU.mult))
        step(dve, lambda e: e.tensor_tensor(C("t1"), C("s1"), col("lc_re"), ALU.mult))
        step(dve, lambda e: e.tensor_tensor(C("zb"), C("t0"), C("t1"), ALU.add))
        step(dve, lambda e: e.tensor_scalar(C("zb"), C("zb"), -1.0, None, ALU.mult))
        t_state = chain[0]
        step(pool, lambda e: e.memset(cosT[:, :, 0:1], 1.0))
        step(pool, lambda e: e.memset(sinT[:, :, 0:1], 0.0))
        step(pool, lambda e: e.tensor_copy(C("pc"), C("c1")))
        step(pool, lambda e: e.tensor_copy(C("ps"), C("s1")))
        n = 1
        while n < SEQ:
            def wide(name, n=n):
                return sm[:, cols[name], :].rearrange("p (l o) -> p l o", o=1).broadcast_to([P, DEPTH, n])
            c0, s0 = cosT[:, :, 0:n], sinT[:, :, 0:n]
            c1, s1 = cosT[:, :, n:2 * n], sinT[:, :, n:2 * n]
            ta, tb = tab[:, :, 0:n], tab2[:, :, 0:n]
            before = chain[0]
            p1 = pool.add(lambda e, c1=c1, c0=c0, w=wide: e.tensor_tensor(c1, c0, w("pc"), ALU.mult), before)
            p2 = pool.add(lambda e, ta=ta, s0=s0, w=wide: e.tensor_tensor(ta, s0, w("ps"), ALU.mult), before)
            p3 = pool.add(lambda e, s1=s1, s0=s0, w=wide: e.tensor_tensor(s1, s0, w("pc"), ALU.mult), before)
            p4 = pool.add(lambda e, tb=tb, c0=c0, w=wide: e.tensor_tensor(tb, c0, w("ps"), ALU.mult), before)
            pool.add(lambda e, c1=c1, ta=ta: e.tensor_tensor(c1, c1, ta, ALU.subtract), p2)
            chain[0] = pool.add(lambda e, s1=s1, tb=tb: e.tensor_tensor(s1, s1, tb, ALU.add), p4)
            n *= 2
            if n < SEQ:
                step(pool, lambda e: e.tensor_tensor(C("pc2"), C("pc"), C("pc"), ALU.mult))
                step(pool, lambda e: e.tensor_tensor(C("t1"), C("ps"), C("ps"), ALU.mult))
                step(pool, lambda e: e.tensor_tensor(C("ps2"), C("pc"), C("ps"), ALU.mult))
                step(pool, lambda e: e.tensor_tensor(C("pc"), C("pc2"), C("t1"), ALU.subtract))
                step(pool, lambda e: e.tensor_tensor(C("ps"), C("ps2"), C("ps2"), ALU.add))
        t_tables = chain[0]

        t_l = act.add(lambda e: e.activation(long_st[0:96, :], long_raw[0:96, :], ACT.Copy), t_lr)
        t_s = act.add(lambda e: e.activation(short_st[0:96, :, :], short_raw[0:96, :, :], ACT.Copy), t_lr)
        dve.add(lambda e: e.tensor_tensor(long_st[32:64, :], long_raw[32:64, :], long_st[32:64, :].bitcast(F32),
                                          ALU.subtract), t_l)
        t_lowrank = dve.add(lambda e: e.tensor_tensor(short_st[64:96, :, :], short_raw[64:96, :, :],
                                                      short_st[64:96, :, :].bitcast(F32), ALU.subtract), t_s)

        hidden = [sl[:, 0], sl[:, 1], F1["gate"], F1["xn"]]
        hidden_free = [t_lowrank, t_lowrank, t_tables, None]

        def stack_stream(s):
            turn_b = [0]

            def bank():
                turn_b[0] += 1
                return 2 * s + turn_b[0] % 2

            hh, cen, sq, ur, yn, act_y = h[s], buf_a[s], buf_b[s], buf_c[s], buf_d[s], buf_e[s]
            zi, ui, rexp, zr = cen, sq, ur, yn
            tiles = list(range(s * TPB, (s + 1) * TPB))
            xT, hid = F1["xT"][s % 2], hidden[s]
            for j, t in enumerate(tiles):
                c_ = slice(j * P, (j + 1) * P)
                t_x = ln_apply(t, rs0[s], F1["xn"], bank(), xT[0][:, :, c_], xT[1][:, :, c_], F1["xT_free"][s % 2])
                x_read[t] = t_x
                yield
            b = bank()
            pairs = []
            for g in range(NG2):
                w_off = DIM * (NG2 - 1 - g)
                pairs += [((win_hi[:, k, w_off:w_off + P], win_lo[:, k, w_off:w_off + P]),
                           (xT[0][:, k, g * SW:(g + 1) * SW], xT[1][:, k, g * SW:(g + 1) * SW])) for k in range(KC)]
            t_h = mm3(psum[:, b, 0:SW], pairs, t_x, t_winr, bank_free[b])
            F1["xT_free"][s % 2] = t_h
            yield
            t_h = dve.add(lambda e: e.tensor_scalar(hh[:], psum[:, b, 0:SW], col("bin"), None, ALU.add), t_h, t_vec)
            bank_free[b] = t_h
            yield

            def norm(t_h):
                b = bank()
                t_c = mm(psum[:, b, 0:SW], center[:], hh[:], True, True, t_h, t_center, bank_free[b], mark=True)
                yield
                t_cc = dve.add(lambda e: e.tensor_copy(cen[:], psum[:, b, 0:SW]), t_c)
                bank_free[b] = t_cc
                yield
                t_sq = act.add(lambda e: e.activation(sq[:], cen[:], ACT.Square), t_cc)
                yield
                b = bank()
                for j in range(SJ):
                    t_v = mm(psum[:, b, j * NG2:(j + 1) * NG2], sq[:, j * P:(j + 1) * P], blk_mean[:], True, True,
                             t_sq, bank_free[b], mark=(j == SJ - 1))
                yield
                t_e = dve.add(lambda e: e.tensor_scalar(svar[:, s, :], psum[:, b, 0:SJ * NG2], LN_EPS, None, ALU.add), t_v)
                bank_free[b] = t_e
                t_r = pool.add(lambda e: e.tensor_tensor(srstd[:, s, :], svar[:, s, :], mneg_half[:, 0:SJ * NG2],
                                                         ALU.pow), t_e, t_half)
                yield
                t_x = dve.add(lambda e: e.tensor_copy(
                    rexp[:].rearrange("p (j d) -> p j d", d=DIM),
                    srstd[:, s, :].rearrange("p (j o) -> p j o", o=1).broadcast_to([P, SJ * NG2, DIM])), t_r)
                yield
                b = bank()
                for j in range(SJ):
                    t_t = pe.add(lambda e: e.transpose(psum[:, b, j * P:(j + 1) * P], rexp[:, j * P:(j + 1) * P],
                                                       ident[:]), t_x, bank_free[b], mark=(j == SJ - 1))
                yield
                t_y = dve.add(lambda e: e.tensor_tensor(yn[:], cen[:], psum[:, b, 0:SW], ALU.mult), t_t)
                bank_free[b] = t_y
                yield
                return t_y

            for l in range(DEPTH):
                t_y = yield from norm(t_h)
                t_a = act.add(lambda e: e.activation(act_y[:], yn[:], ACT.Silu, bias=col("ln1_b", l),
                                                     scale=col("ln1_w", l)), t_y)
                yield
                cw, sw = cosT[:, l, :], sinT[:, l, :]
                t_ui = pool.add(lambda e: e.tensor_tensor(ui[:], act_y[:], sw, ALU.mult), t_a, t_tables)
                t_ur = dve.add(lambda e: e.tensor_tensor(ur[:], act_y[:], cw, ALU.mult), t_a, t_tables)
                yield
                rho = sm[:, cols["rho"], l:l + 1].broadcast_to([P, SW])
                t_zr = dve.add(lambda e: e.tensor_tensor_scan(zr[:], rho, ur[:], sm[:, cols["za"], l:l + 1],
                                                              ALU.mult, ALU.add), t_ur, t_state)
                yield
                t_zi = dve.add(lambda e: e.tensor_tensor_scan(zi[:], rho, ui[:], sm[:, cols["zb"], l:l + 1],
                                                              ALU.mult, ALU.add), t_ui, t_state)
                t_pi = pool.add(lambda e: e.tensor_tensor(ui[:], zi[:], sw, ALU.mult), t_zi)
                t_pr = dve.add(lambda e: e.tensor_tensor(ur[:], zr[:], cw, ALU.mult), t_zr)
                yield
                t_h = dve.add(lambda e: e.scalar_tensor_tensor(out=hh[:], in0=ur[:], scalar=col("sc_lin", l), in1=hh[:],
                                                               op0=ALU.mult, op1=ALU.add), t_pr)
                yield
                t_h = dve.add(lambda e: e.scalar_tensor_tensor(out=hh[:], in0=ui[:], scalar=col("sc_lin", l), in1=hh[:],
                                                               op0=ALU.mult, op1=ALU.add), t_h, t_pi)
                yield
                t_y = yield from norm(t_h)
                t_y2 = dve.add(lambda e: e.tensor_scalar(act_y[:], yn[:], col("ln2_w", l), col("ln2_b", l),
                                                         ALU.mult, ALU.add), t_y)
                t = tiles[l]
                x_ready[t] = pool.add(lambda e: e.tensor_tensor(x[:, t, :], x[:, t, :], bout_sb[:], ALU.add),
                                      x_read[t], t_small)
                yield
                t_sl = []
                banks2 = slice(2 * s, 2 * s + 2)
                for c in range(DFF // P):
                    for g in range(NG2):
                        rows = slice(g * DIM, (g + 1) * DIM)
                        t_m = mm(psum[:, 2 * s + g, c * SW:(c + 1) * SW], w1_sb[rows, l, c * P:(c + 1) * P],
                                 act_y[rows, :], True, True, t_y2, t_small, bank_free[2 * s], bank_free[2 * s + 1],
                                 mark=(c == DFF // P - 1))
                        last = [t_m] if g == 0 else last + [t_m]
                yield
                for c in range(DFF // P):
                    t_sl.append(act.add(lambda e: e.activation(
                        hid[:, c, :].rearrange("p (g t) -> p g t", g=NG2), psum[:, banks2, c * SW:(c + 1) * SW],
                        ACT.Silu, bias=b1_sb[:, l, c:c + 1]), last, hidden_free[s], xn_users))
                    yield
                bank_free[2 * s] = bank_free[2 * s + 1] = t_sl[-1]
                b = bank()
                n = 0
                for c in range(DFF // P):
                    for g in range(NG2):
                        off = DIM * (NG2 - 1 - g)
                        n += 1
                        t_m = mm(psum[:, b, 0:SW], w2_sb[:, l * (DFF // P) + c, off:off + P],
                                 hid[:, c, g * SW:(g + 1) * SW], n == 1, n == NG2 * (DFF // P), t_sl[c], bank_free[b],
                                 mark=(n == NG2 * (DFF // P)))
                hidden_free[s] = t_m
                yield
                t_h = dve.add(lambda e: e.scalar_tensor_tensor(out=hh[:], in0=psum[:, b, 0:SW], scalar=col("b2", l),
                                                               in1=hh[:], op0=ALU.add, op1=ALU.add), t_m)
                bank_free[b] = t_h
                yield
            t_y = yield from norm(t_h)
            t_y2 = dve.add(lambda e: e.tensor_scalar(act_y[:], yn[:], col("lnl_w"), col("lnl_b"), ALU.mult, ALU.add),
                           t_y)
            yield
            for n, t in enumerate(tiles):
                g, j = divmod(n, SJ)
                rows = slice(g * DIM, (g + 1) * DIM)
                b = bank()
                t_m = mm(psum[:, b, :], act_y[rows, j * P:(j + 1) * P], wout_sb[rows, :], True, True, t_y2,
                         bank_free[b], mark=True)
                yield
                x_ready[t] = dve.add(lambda e: e.tensor_tensor(x[:, t, :], x[:, t, :], psum[:, b, :], ALU.add),
                                     t_m, x_ready[t])
                bank_free[b] = x_ready[t]
            yield

        GATE, UP, AUX = 4, 5, (6, 7)
        weff_slot = [Slot(sem(f"weff_out{i}")) for i in range(2)]
        weff_saved = [None] * IC

        def ffn(F, make_weff, prep, buffers_free=None, finished=None):
            nseq = NBLK * IC
            wgu_free, wdn_free = [None] * 2, [None] * 3
            gate_free, dT_free, weff_free = [buffers_free] * 2, [None, None], [None]
            d_free = [None]
            aux_turn = [0]

            def fetch(n):
                T, i = divmod(n, IC)
                src = ffn_w[i] if make_weff and T == 0 else weff_dram[i]
                return stage_slot[n % 2].dma(sp, stage[:, n % 2, :], src, stage_free[n % 2],
                                                None if make_weff and T == 0 else weff_saved[i])

            def weights(n, t_raw):
                T, i = divmod(n, IC)
                raw, s, sd = stage[:, n % 2, :], n % 2, n % 3

                def split_both(src, *w):
                    t = split(src[:, 0:2 * DM], F["wgu"][s][0][:], F["wgu"][s][1][:], *w, wgu_free[s])
                    return [t, split(src[:, 2 * DM:], F["wdn"][sd][0][:], F["wdn"][sd][1][:], *w, wdn_free[sd])]
                if not (make_weff and T == 0):
                    stage_free[s] = split_both(raw, t_raw)
                    return stage_free[s]
                cols_ = slice(i * P, (i + 1) * P)
                for kind in range(3):
                    b = AUX[aux_turn[0] % 2]
                    aux_turn[0] += 1
                    if kind < 2:
                        for k in range(KC):
                            t_m = mm(psum[:, b, k * P:(k + 1) * P], short_st[0:96, kind, k * P:(k + 1) * P],
                                     long_st[0:96, cols_], True, True, t_lowrank, bank_free[b], mark=(k == KC - 1))
                    else:
                        t_m = mm(psum[:, b, :], long_st[0:96, cols_], short_st[0:96, kind, :], True, True, t_lowrank,
                                 bank_free[b], mark=True)
                    part = slice(kind * DM, (kind + 1) * DM)
                    t_w = dve.add(lambda e, b=b, part=part: e.tensor_tensor(weff[:, part], raw[:, part], psum[:, b, :],
                                                                            ALU.mult), t_m, t_raw, weff_free[0])
                    bank_free[b] = t_w
                stage_free[s] = t_w
                t = split_both(weff[:], t_w)
                weff_saved[i] = weff_slot[i % 2].dma(sp, weff_dram[i], weff[:], t_w, weff_saved[i - 2] if i >= 2 else None)
                weff_free[0] = [t, weff_saved[i]]
                return t

            t_raw = {n: fetch(n) for n in range(2)}
            t_w = {0: weights(0, t_raw[0])}
            yield
            first = prep(0)
            t_xT = None
            while t_xT is None:
                try:
                    next(first)
                except StopIteration as stop:
                    t_xT = stop.value
            yield
            down = None
            for T in range(NBLK):
                xT = F["xT"][T % 2]
                ahead = prep(T + 1) if T + 1 < NBLK else iter(())
                t_next = None
                for i in range(IC):
                    n = T * IC + i
                    s = n % 2
                    w, wd = F["wgu"][s], F["wdn"][n % 3]
                    if n + 1 < nseq:
                        t_w[n + 1] = weights(n + 1, t_raw[n + 1]) if n + 1 in t_raw else None
                    if n + 2 < nseq:
                        t_raw[n + 2] = fetch(n + 2)
                    for bank_, off in ((GATE, 0), (UP, DM)):
                        pairs = [((w[0][:, off + k * P:off + (k + 1) * P], w[1][:, off + k * P:off + (k + 1) * P]),
                                  (xT[0][:, k, :], xT[1][:, k, :])) for k in range(KC)]
                        t_m = mm3(psum[:, bank_, :], pairs, t_w[n], t_xT, bank_free[bank_])
                        if bank_ == GATE:
                            t_g = act.add(lambda e, s=s: e.activation(F["gate"][:, s, :], psum[:, GATE, :], ACT.Silu),
                                          t_m, gate_free[s])
                            bank_free[GATE] = t_g
                    if i == IC - 1:
                        F["xT_free"][T % 2] = t_m
                    wgu_free[s] = t_m
                    t_d = dve.add(lambda e, s=s: e.tensor_tensor(F["d"][:], F["gate"][:, s, :], psum[:, UP, :], ALU.mult),
                                  t_m, t_g, d_free[0])
                    bank_free[UP] = t_d
                    gate_free[s] = t_d
                    t_ds = split(F["d"][:], F["dT"][s][0][:], F["dT"][s][1][:], t_d, dT_free[s])
                    d_free[0] = t_ds
                    if down:
                        down()

                    def down(T=T, i=i, s=s, t_ds=t_ds, wd=wd, sd=n % 3):
                        for j in range(TPB):
                            c_ = slice(j * P, (j + 1) * P)
                            pairs = [((F["dT"][s][0][:, c_], F["dT"][s][1][:, c_]), (wd[0][:], wd[1][:]))]
                            t_m = mm3(psum[:, j, :], pairs, t_ds, bank_free[j] if i == 0 else None,
                                      start=(i == 0), stop=(i == IC - 1))
                            if i == IC - 1:
                                t = T * TPB + j
                                x_ready[t] = dve.add(lambda e, t=t, j=j: e.tensor_tensor(
                                    x[:, t, :], x[:, t, :], psum[:, j, :], ALU.add), t_m, x_ready[t])
                                bank_free[j] = x_ready[t]
                        wdn_free[sd] = dT_free[s] = t_m
                        if i == IC - 1 and finished:
                            finished(T)
                    if t_next is None:
                        try:
                            next(ahead)
                        except StopIteration as stop:
                            t_next = stop.value
                    yield
                while t_next is None and T + 1 < NBLK:
                    try:
                        next(ahead)
                    except StopIteration as stop:
                        t_next = stop.value
                t_xT = t_next
            down()

        def block_norm(F, T):
            tiles = list(range(T * TPB, (T + 1) * TPB))
            rs = ln_stats(tiles)
            yield
            xT = F["xT"][T % 2]
            for j, t in enumerate(tiles):
                c_ = slice(j * P, (j + 1) * P)
                t_x = ln_apply(t, rs, F["xn"], AUX[j % 2], xT[0][:, :, c_], xT[1][:, :, c_], F["xT_free"][T % 2])
                yield
            return t_x

        def in_turn(streams, apart):
            live, turn = list(enumerate(streams)), 0
            while live:
                for n, g in list(live):
                    if turn >= n * apart and next(g, "end") == "end":
                        live.remove((n, g))
                turn += 1

        streams = [stack_stream(s_) for s_ in range(NS)]
        stage_free[1] = t_lowrank
        for pair in (streams[0:2], streams[2:4]):
            for _ in range(TPB + 2):
                for g in pair:
                    next(g)
        ffn1 = ffn(F1, True, lambda T: block_norm(F1, T), buffers_free=hidden_free)
        next(ffn1)
        in_turn(streams, apart=STEPS_APART)
        xn_users[:] = [list(hidden_free)] * 2
        for _ in ffn1:
            pass

        KVQ = 2 * HD + GRP * HD

        def load_halves(src):
            half = src.shape[-1] // 2
            return [stage_slot[n].dma(sp, stage[:, n, 0:half], src[:, n * half:(n + 1) * half], stage_free[n])
                    for n in range(2)]

        t_kvq_raw = load_halves(wqkv[0])
        marks = barrier(*weff_saved)
        phase1.close()

        phase2 = ExitStack()

        def sb2(name, shape, dt=F32):
            return sb(name, shape, dt, phase2)
        axT = [sb2(f"axT_{p}", [P, KC, TOK], F32R) for p in "hl"]
        wkvq = [sb2(f"wkvq_{p}", [P, KC, KVQ], F32R) for p in "hl"]
        wo_s = [sb2(f"wo_{p}", [P, GRP, DM], F32R) for p in "hl"]
        qT = [sb2(f"qT_{p}", [P, GRP, SEQ], F32R) for p in "hl"]
        kT = [sb2(f"kT_{p}", [P, SEQ], F32R) for p in "hl"]
        vv = [[sb2(f"v{s}_{p}", [P, STILES, HD], F32R) for p in "hl"] for s in range(2)]
        oT = [sb2(f"oT_{p}", [P, GRP, SEQ], F32R) for p in "hl"]
        q_tok = sb2("q_tok", [P, STILES, GRP * HD])
        k_tok = sb2("k_tok", [P, STILES, HD])
        squares = sb2("squares", [P, GRP * HD])
        SC = P + SEQ
        biased = sb2("biased", [P, 2, SC])
        prob = sb2("prob", [P, GRP, SC])
        pT = [sb2(f"pT_{p}", [P, 2, SC], F32R) for p in "hl"]
        xn_a = sb2("xn_a", [P, DM])
        alibi = sb2("alibi", [P, GRP, SC])
        rel = sb2("rel", [P, SC])
        future = sb2("future", [P, SC])
        qkw = sb2("qkw", [P, 2, HD])
        kw = sb2("kw", [P, HD])
        ss_q = sb2("ss_q", [P, STILES, GRP])
        r_q = sb2("r_q", [P, STILES, GRP])
        ss_k = sb2("ss_k", [P, STILES])
        r_k = sb2("r_k", [P, STILES])
        nmax = sb2("nmax", [P, GRP, STILES])
        esum = sb2("esum", [P, GRP, STILES])
        rsum = sb2("rsum", [P, GRP, STILES])
        KV, QB, WO = 4, (5, 6), 7

        t_qkw = Slot(sem("qkw_in")).dma(sp, qkw[:], qk_w.partition_broadcast(P), marks)
        t_kw = dve.add(lambda e: e.tensor_tensor(kw[:], qkw[:, 0, :], qkw[:, 1, :], ALU.mult), t_qkw)
        pool.add(lambda e: e.iota(rel[:, 0:P], [[1, P]], base=0, channel_multiplier=-1,
                                  allow_small_or_imprecise_dtypes=True))
        t_rel = pool.add(lambda e: e.iota(rel[:, P:], [[1, SEQ]], base=-P, channel_multiplier=-1,
                                          allow_small_or_imprecise_dtypes=True))
        t_fut = dve.add(lambda e: e.tensor_scalar(future[:], rel[:], 0.0, NEG_INF, ALU.is_gt, ALU.mult), t_rel)

        ready_w = {}
        free_w = {"kv": None, "q": None, "wo": None}

        def split_kv(t_raw):
            src = stage[:].rearrange("p a (k n) -> p (a k) n", n=KVQ)[:, :, 0:2 * HD]
            ready_w["kv"] = split(src, wkvq[0][:, :, 0:2 * HD], wkvq[1][:, :, 0:2 * HD], t_raw, free_w["kv"], on=pool)

        def split_q(half, t_raw):
            k = slice(half * KC // 2, (half + 1) * KC // 2)
            src = stage[:, half, :].rearrange("p (k n) -> p k n", n=KVQ)[:, :, 2 * HD:]
            ready_w["q", half] = split(src, wkvq[0][:, k, 2 * HD:], wkvq[1][:, k, 2 * HD:], t_raw[half], free_w["q"], on=pool)
            stage_free[half] = [ready_w["kv"], ready_w["q", half]]

        def split_wo(half, t_raw):
            hs = slice(half * GRP // 2, (half + 1) * GRP // 2)
            src = stage[:, half, 0:GRP // 2 * DM].rearrange("p (h n) -> p h n", n=DM)
            ready_w["wo", half] = split(src, wo_s[0][:, hs, :], wo_s[1][:, hs, :], t_raw[half], free_w["wo"], on=pool)
            stage_free[half] = ready_w["wo", half]

        rs = [ln_stats(list(range(T * TPB, (T + 1) * TPB))) for T in range(NBLK)]
        t_ax = [None] * NT
        xn_read = [None]
        t_xn = [None]

        def norm_rows(t):
            t_xn[0] = dve.add(lambda e: e.tensor_scalar(xn_a[:], x[:, t, :], ln_mv[:, t, 0:1], ln_rstd[:, t:t + 1],
                                                        ALU.subtract, ALU.mult), rs[t // TPB], xn_read[0])

        def norm_transpose(t, bank=WO):
            for k in range(KC):
                t_tr = pe.add(lambda e: e.transpose(psum[:, bank, k * P:(k + 1) * P], xn_a[:, k * P:(k + 1) * P],
                                                    ident[:]), t_xn[0], bank_free[bank], mark=(k == KC - 1))
            xn_read[0] = t_tr
            c_ = slice(t * P, (t + 1) * P)
            t_ax[t] = bank_free[bank] = split(psum[:, bank, :].rearrange("p (k c) -> p k c", k=KC),
                                              axT[0][:, :, c_], axT[1][:, :, c_], t_tr)

        t_al, al_free = [None] * GRP, [None] * GRP

        def alibi_table(g, hd):
            t_al[hd] = dve.add(lambda e: e.scalar_tensor_tensor(
                out=alibi[:, hd, :], in0=rel[:], scalar=SLOPES[g * GRP + hd], in1=future[:],
                op0=ALU.mult, op1=ALU.add), t_fut, al_free[hd])

        ft = {"v": [None, None], "kT": None, "qT": None, "k_tok": None, "q_tok": [None, None], "oT": None,
              "biased": [None, None], "prob": [None] * GRP, "pT": None, "sq": None}
        tk = {}

        def kv_proj(u):
            g, b = divmod(u, BATCH)
            s = u % 2
            for t in range(STILES):
                tile = b * STILES + t
                c_ = slice(tile * P, (tile + 1) * P)
                pairs = [((axT[0][:, k, c_], axT[1][:, k, c_]), (wkvq[0][:, k, 0:2 * HD], wkvq[1][:, k, 0:2 * HD]))
                         for k in range(KC)]
                t_m = mm3(psum[:, KV, t * 2 * HD:(t + 1) * 2 * HD], pairs, t_ax[tile], ready_w["kv"], bank_free[KV])
            if b == BATCH - 1:
                free_w["kv"] = t_m
            kv = psum[:, KV, :].rearrange("p (t n) -> p t n", t=STILES)
            for t in range(STILES):
                t_ss = act.add(lambda e, t=t: e.activation(squares[:, t * HD:(t + 1) * HD], kv[:, t, 0:HD], ACT.Square,
                                                           accum_out=ss_k[:, t:t + 1]), t_m, ft["sq"], ft["k_tok"])
            ft["sq"] = t_ss
            t_a = pool.add(lambda e: e.tensor_scalar(ss_k[:], ss_k[:], 1.0 / HD, RMS_EPS, ALU.mult, ALU.add), t_ss)
            t_r = pool.add(lambda e: e.tensor_tensor(r_k[:], ss_k[:], mneg_half[:, 0:STILES], ALU.pow), t_a)
            tk["v"] = split(kv[:, :, HD:2 * HD], vv[s][0][:], vv[s][1][:], t_m, ft["v"][s])
            tk["kr"] = t_r

        def k_scale(u):
            kv = psum[:, KV, :].rearrange("p (t n) -> p t n", t=STILES)
            for t in range(STILES):
                t_k = dve.add(lambda e, t=t: e.scalar_tensor_tensor(out=k_tok[:, t, :], in0=kv[:, t, 0:HD],
                                                                    scalar=r_k[:, t:t + 1], in1=kw[:], op0=ALU.mult,
                                                                    op1=ALU.mult), tk["kr"], t_kw, ft["k_tok"])
            bank_free[KV] = [tk["v"], t_k]
            tk["k"] = t_k

        def k_transpose(u):
            for t in range(STILES):
                t_t = pe.add(lambda e, t=t: e.transpose(psum[:, KV, t * P:(t + 1) * P], k_tok[:, t, :], ident[:]),
                             tk["k"], bank_free[KV], mark=(t == STILES - 1))
            ft["k_tok"] = t_t
            tk["kT"] = bank_free[KV] = split(psum[:, KV, 0:SEQ], kT[0][:], kT[1][:], t_t, ft["kT"])

        def q_proj(u, t):
            g, b = divmod(u, BATCH)
            tile = b * STILES + t
            c_ = slice(tile * P, (tile + 1) * P)
            for half in range(2):
                pairs = [((axT[0][:, k, c_], axT[1][:, k, c_]), (wkvq[0][:, k, 2 * HD:], wkvq[1][:, k, 2 * HD:]))
                         for k in range(half * KC // 2, (half + 1) * KC // 2)]
                t_m = mm3(psum[:, QB[t], :], pairs, t_ax[tile], ready_w["q", half], bank_free[QB[t]],
                          start=(half == 0), stop=(half == 1))
            if b == BATCH - 1:
                free_w["q"] = t_m
            t_sq = act.add(lambda e: e.activation(squares[:], psum[:, QB[t], :], ACT.Square), t_m, ft["sq"])
            t_ss = dve.add(lambda e: e.tensor_reduce(ss_q[:, t, :], squares[:].rearrange("p (h d) -> p h d", h=GRP),
                                                     AX.X, ALU.add), t_sq, ft["q_tok"][t])
            ft["sq"] = t_ss
            t_a = pool.add(lambda e: e.tensor_scalar(ss_q[:, t, :], ss_q[:, t, :], 1.0, HD * RMS_EPS, ALU.mult, ALU.add),
                           t_ss)
            t_r = pool.add(lambda e: e.tensor_tensor(r_q[:, t, :], ss_q[:, t, :], mneg_half[:, 0:GRP], ALU.pow), t_a)
            tk["qr", t] = t_r

        def q_scale(u, t):
            t_q = dve.add(lambda e: e.tensor_tensor(
                q_tok[:, t, :].rearrange("p (h d) -> p h d", h=GRP),
                psum[:, QB[t], :].rearrange("p (h d) -> p h d", h=GRP),
                r_q[:, t, :].rearrange("p (h o) -> p h o", o=1).broadcast_to([P, GRP, HD]), ALU.mult),
                tk["qr", t], ft["q_tok"][t])
            bank_free[QB[t]] = t_q
            tk["q", t] = t_q

        def q_transpose(u, t):
            for hd in range(GRP):
                t_t = pe.add(lambda e, hd=hd: e.transpose(psum[:, QB[t], hd * P:(hd + 1) * P],
                                                          q_tok[:, t, hd * HD:(hd + 1) * HD], ident[:]),
                             tk["q", t], bank_free[QB[t]], mark=(hd == GRP - 1))
            ft["q_tok"][t] = t_t
            c_ = slice(t * P, (t + 1) * P)
            tk["qT", t] = bank_free[QB[t]] = split(psum[:, QB[t], :].rearrange("p (h c) -> p h c", h=GRP),
                                                   qT[0][:, :, c_], qT[1][:, :, c_], t_t, ft["qT"])

        def scores(u, hd):
            s = hd % 2
            part = ((0, P), (P, SC))
            for t in range(STILES):
                a, b_ = part[t]
                q_ = slice(t * P, (t + 1) * P)
                pairs = [((qT[0][:, hd, q_], qT[1][:, hd, q_]), (kT[0][:, 0:b_ - a], kT[1][:, 0:b_ - a]))]
                t_m = mm3(psum[:, hd, a:b_], pairs, tk["qT", t], tk["kT"], bank_free[hd])
            ft["qT"] = ft["kT"] = t_m
            for t in range(STILES):
                a, b_ = part[t]
                t_b = dve.add(lambda e, t=t, a=a, b_=b_: e.tensor_tensor_reduce(
                    biased[:, s, a:b_], psum[:, hd, a:b_], alibi[:, hd, a:b_], -1.0, 3e38, ALU.add, ALU.min,
                    nmax[:, hd, t:t + 1]), t_m, t_al[hd], ft["biased"][s])
                t_e = act.add(lambda e, t=t, a=a, b_=b_: e.activation(
                    prob[:, hd, a:b_], biased[:, s, a:b_], ACT.Exp, bias=nmax[:, hd, t:t + 1], scale=-1.0,
                    accum_out=esum[:, hd, t:t + 1]), t_b, ft["prob"][hd])
            bank_free[hd] = al_free[hd] = t_b
            ft["biased"][s] = tk["e", hd] = t_e

        def normalise(hd):
            part = ((0, P), (P, SC))
            t_r = dve.add(lambda e: e.reciprocal(rsum[:, hd, :], esum[:, hd, :]), tk["e", hd])
            for t in range(STILES):
                a, b_ = part[t]
                t_p = pool.add(lambda e, t=t, a=a, b_=b_: e.tensor_scalar(prob[:, hd, a:b_], prob[:, hd, a:b_],
                                                                          rsum[:, hd, t:t + 1], 1.0, ALU.mult, ALU.mult), t_r)
            tk["p", hd] = t_p

        def p_transpose(u, hd):
            s = hd % 2
            for n in range(SC // P):
                t_t = pe.add(lambda e: e.transpose(psum[:, hd, n * P:(n + 1) * P], prob[:, hd, n * P:(n + 1) * P],
                                                   ident[:]), tk["p", hd], bank_free[hd], mark=(n == SC // P - 1))
            ft["prob"][hd] = t_t
            tk["pT", hd] = bank_free[hd] = split(psum[:, hd, 0:SC], pT[0][:, s, :], pT[1][:, s, :], t_t, ft["pT"])

        def attend(u, pair):
            v = vv[u % 2]
            b = 2 * pair
            both = psum[:, b, :].rearrange("p (h c) -> p h c", h=2)
            mm3(both, [((v[0][:, 0, :], v[1][:, 0, :]), (pT[0][:, :, 0:SEQ], pT[1][:, :, 0:SEQ]))],
                tk["pT", b], tk["pT", b + 1], tv[u % 2], bank_free[b], stop=False)
            t_m = mm3(both[:, :, P:SEQ], [((v[0][:, 1, :], v[1][:, 1, :]), (pT[0][:, :, SEQ:], pT[1][:, :, SEQ:]))],
                      start=False)
            ft["pT"] = t_m
            ft["v"][u % 2] = t_m
            tk["oT", pair] = bank_free[b] = split(both, oT[0][:, b:b + 2, :], oT[1][:, b:b + 2, :], t_m, ft["oT"])

        def out_proj(u, t):
            g, b = divmod(u, BATCH)
            tile = b * STILES + t
            c_ = slice(t * P, (t + 1) * P)
            bank = (1, WO)[t]
            pe.wait(bank_free[bank])
            for hd in range(GRP):
                t_m = mm3(psum[:, bank, :], [((oT[0][:, hd, c_], oT[1][:, hd, c_]), (wo_s[0][:, hd, :], wo_s[1][:, hd, :]))],
                          tk["oT", hd // 2], ready_w["wo", hd // (GRP // 2)], start=(hd == 0), stop=(hd == GRP - 1))
            if t == STILES - 1:
                ft["oT"] = t_m
                if b == BATCH - 1:
                    free_w["wo"] = t_m
            x_ready[tile] = dve.add(lambda e: e.tensor_tensor(x[:, tile, :], x[:, tile, :], psum[:, bank, :], ALU.add),
                                    t_m, x_ready[tile])
            bank_free[bank] = x_ready[tile]

        tv = [None, None]
        units = KVH * BATCH
        ahead = 2
        split_kv(t_kvq_raw)
        norm_rows(0)
        norm_transpose(0, QB[0])
        norm_rows(1)
        norm_transpose(1, QB[1])
        kv_proj(0)
        tv[0] = tk["v"]
        k_scale(0)
        for half in range(2):
            split_q(half, t_kvq_raw)
        t_wo_raw = load_halves(wo[0])
        for hd in range(GRP):
            alibi_table(0, hd)
        for t in range(STILES):
            q_proj(0, t)
            norm_rows(STILES + t)
            norm_transpose(STILES + t)
            q_scale(0, t)
        k_transpose(0)
        for t in range(STILES):
            q_transpose(0, t)
        for u in range(units):
            g, b = divmod(u, BATCH)
            nxt = u + 1 < units
            last_proj = b == BATCH - 2 and g + 1 < KVH
            fresh = [t for t in range((u + ahead) * STILES, (u + ahead + 1) * STILES) if t < NT]
            for hd in range(GRP):
                scores(u, hd)
                if b == BATCH - 1 and nxt:
                    alibi_table(g + 1, hd)
                if hd > 0:
                    normalise(hd - 1)
            normalise(GRP - 1)
            if fresh:
                norm_rows(fresh[0])
            if nxt:
                kv_proj(u + 1)
                tv[(u + 1) % 2] = tk["v"]
            if b == 0:
                split_wo(0, t_wo_raw)
            p_transpose(u, 0)
            p_transpose(u, 1)
            if nxt:
                k_scale(u + 1)
            if fresh:
                norm_transpose(fresh[0])
                norm_rows(fresh[1])
            if nxt:
                q_proj(u + 1, 0)
            if last_proj:
                split_kv(t_kvq_raw)
            if b == 0:
                split_wo(1, t_wo_raw)
                if g + 1 < KVH:
                    t_kvq_raw = load_halves(wqkv[g + 1])
            attend(u, 0)
            p_transpose(u, 2)
            p_transpose(u, 3)
            if nxt:
                q_scale(u + 1, 0)
            if fresh:
                norm_transpose(fresh[1])
            if nxt:
                q_proj(u + 1, 1)
            if last_proj:
                split_q(0, t_kvq_raw)
            attend(u, 1)
            if nxt:
                q_scale(u + 1, 1)
                k_transpose(u + 1)
                q_transpose(u + 1, 0)
            if last_proj:
                split_q(1, t_kvq_raw)
                t_wo_raw = load_halves(wo[g + 1])
            out_proj(u, 0)
            if nxt:
                q_transpose(u + 1, 1)
            out_proj(u, 1)
        barrier()
        phase2.close()

        phase3 = ExitStack()
        F2 = ffn_buffers(phase3, "b")
        xn_users[:] = [None, None]
        ov = out.rearrange("(t p) d -> p t d", p=P)
        stored = []

        def store(T):
            tiles = range(T * TPB, (T + 1) * TPB)
            if T < NBLK - 1:
                stored.append(Slot(sem(f"x_out{T}")).dma(
                    sp, ov[:, tiles[0]:tiles[-1] + 1, :], x[:, tiles[0]:tiles[-1] + 1, :], x_ready[tiles[-1]]))
            else:
                for t in tiles:
                    stored.append(Slot(sem(f"x_out_tile{t}")).dma(sp, ov[:, t, :], x[:, t, :], x_ready[t]))

        for _ in ffn(F2, False, lambda T: block_norm(F2, T), finished=store):
            pass
        sp.wait(*stored)
        phase3.close()


def kernel(**inputs):
    import concourse.bacc as bacc
    from concourse.bass_utils import run_bass_kernel_spmd

    a = {n[3:]: np.asarray(v) for n, v in inputs.items()}
    x = a["attn_a_x"].reshape(TOK, DM)
    win = a["attn_a_Win"].T
    vecs = np.concatenate([a["attn_a_" + n].T.reshape(DIM, w) for n, (_, w) in VEC.items()], axis=1)
    b1 = a["attn_a_b1"].reshape(DEPTH, DFF // P, P).transpose(2, 0, 1)
    w1 = a["attn_a_W1"].transpose(2, 0, 1)
    w2 = a["attn_a_W2"].transpose(0, 2, 1).reshape(DEPTH, DFF // P, P, DIM).transpose(2, 0, 1, 3).reshape(P, -1, DIM)
    wout = a["attn_a_Wout"].T

    def in_out(w):
        return w.reshape(IC, P, KC, P).transpose(0, 3, 2, 1).reshape(IC, P, DM)
    ffn_w = np.concatenate([in_out(a["ffn_gate_w"]), in_out(a["ffn_up_w"]),
                            a["ffn_down_w"].T.reshape(IC, P, DM)], axis=2)
    lr_long = np.concatenate([a["ffn_gate_su"].T, a["ffn_up_su"].T, a["ffn_down_sv"]], axis=0)
    lr_short = np.concatenate([a["ffn_gate_sv"], a["ffn_up_sv"], a["ffn_down_su"].T], axis=0)

    def by_group(w, n):
        return w.reshape(KVH, n, KC, P).transpose(0, 3, 2, 1)
    wqkv = np.concatenate([by_group(a["attn_b_Wk"], HD), by_group(a["attn_b_Wv"], HD),
                           by_group(a["attn_b_Wq"], GRP * HD)], axis=3).reshape(KVH, P, -1)
    wo = a["attn_b_Wo"].reshape(DM, KVH, GRP, HD).transpose(1, 3, 2, 0).reshape(KVH, HD, -1)
    qk_w = np.stack([a["attn_b_q_norm_w"], a["attn_b_k_norm_w"]])

    nc = bacc.Bacc("TRN2", target_bir_lowering=False, num_devices=1)
    arrays, args = {}, []
    for name, v in (("x", x), ("win", win), ("vecs", vecs), ("b1", b1), ("w1", w1), ("w2", w2), ("wout", wout),
                    ("bout", a["attn_a_bout"]), ("ffn_w", ffn_w), ("lr_long", lr_long), ("lr_short", lr_short),
                    ("wqkv", wqkv), ("wo", wo), ("qk_w", qk_w)):
        name = "in_" + name
        arrays[name] = np.ascontiguousarray(v)
        args.append(nc.dram_tensor(name, arrays[name].shape, F32, kind="ExternalInput").ap())
    args.append(nc.dram_tensor("out", (TOK, DM), F32, kind="ExternalOutput").ap())
    args.append(nc.dram_tensor("weff_dram", (IC, P, 3 * DM), F32, kind="Internal").ap())
    hybrid_block(nc, *args)
    r = run_bass_kernel_spmd(nc, [arrays], core_ids=[0])
    return r.results[0]["out"].reshape(BATCH, SEQ, DM)
```

```python
from contextlib import ExitStack
import math

import numpy as np

import concourse.bass as bass
from concourse import mybir

F32 = mybir.dt.float32
F32R = mybir.dt.float32r
ALU = mybir.AluOpType
ACT = mybir.ActivationFunctionType
AX = mybir.AxisListType

P = 128
BATCH, SEQ, DM = 8, 256, 512
TOK = BATCH * SEQ
NT = TOK // P
KC = DM // P
BLK = 512
TPB = BLK // P
NBLK = TOK // BLK
DEPTH, DIM, DFF = 4, 64, 256
NG2 = P // DIM
INNER, RANK = 1792, 4
IC = INNER // P
HEADS, KVH, HD = 32, 8, 128
GRP = HEADS // KVH
STILES = SEQ // P
LN_EPS, RMS_EPS = 1e-5, 1e-6
NEG_INF = -1e30
SLOPE0 = 2 ** (-2 ** (-(math.log2(HEADS) - 3)))
SLOPES = [float(np.float32(SLOPE0 * SLOPE0 ** i)) for i in range(HEADS)]

VEC = {}
for _n, _w in (("ln1_w", DEPTH), ("ln1_b", DEPTH), ("phz_re", DEPTH), ("phz_im", DEPTH), ("lc_re", DEPTH),
               ("lc_im", DEPTH), ("sc_lin", DEPTH), ("ln2_w", DEPTH), ("ln2_b", DEPTH), ("b2", DEPTH),
               ("bin", 1), ("lnl_w", 1), ("lnl_b", 1)):
    VEC[_n] = (sum(w for _, w in VEC.values()), _w)
NVEC = sum(w for _, w in VEC.values())

PASSES = ((0, 0), (0, 1), (1, 0))


class Lane:

    def __init__(self, engine, sem):
        self.engine, self.sem, self.count, self.seen = engine, sem, 0, {}

    def wait(self, *tickets):
        for t in tickets:
            if t is None:
                continue
            if isinstance(t, list):
                self.wait(*t)
                continue
            sem, value = t
            if self.seen.get(id(sem), 0) < value:
                self.seen[id(sem)] = value
                self.engine.wait_ge(sem, value)

    def add(self, fn, *waits, mark=True):
        self.wait(*waits)
        ins = fn(self.engine)
        if not mark:
            return None
        ins.then_inc(self.sem, 1)
        self.count += 1
        return (self.sem, self.count)

    def now(self):
        return (self.sem, self.count) if self.count else None


class Slot:

    def __init__(self, sem):
        self.sem, self.count = sem, 0

    def dma(self, lane, dst, src, *waits):
        lane.wait(*waits)
        self.count += 16
        lane.engine.dma_start(dst, src).then_inc(self.sem, 16)
        return (self.sem, self.count)


def hybrid_block(nc, x_in, win, vecs, b1, w1, w2, wout, bout, ffn_w, lr_long, lr_short, wqkv, wo, qk_w, out, weff_dram):
    with ExitStack() as ctx:
        def sb(name, shape, dt=F32, stack=None):
            return (stack or ctx).enter_context(nc.sbuf_tensor(name, shape, dt))

        def sem(name):
            return ctx.enter_context(nc.semaphore(name))

        pe, act, dve, pool, sp = (Lane(engine, sem(name)) for engine, name in (
            (nc.tensor, "pe_done"), (nc.scalar, "act_done"), (nc.vector, "dve_done"), (nc.gpsimd, "pool_done"),
            (nc.sync, "sp_done")))
        psum = ctx.enter_context(nc.psum_tensor("psum", [P, 8, 512], F32))
        bank_free = [None] * 8

        x = sb("x", [P, NT, DM])
        ident = sb("ident", [P, P])
        mneg_half = sb("mneg_half", [P, 16])
        ln_mv = sb("ln_mv", [P, NT, 2])
        ln_bn = sb("ln_bn", [P, 2, 6])
        ln_var = sb("ln_var", [P, NT])
        ln_rstd = sb("ln_rstd", [P, NT])
        x_ready = [None] * NT
        stage = sb("stage", [P, 2, 3 * DM])
        stage_slot = [Slot(sem(f"stage{i}")) for i in range(3)]
        stage_free = [None, None, None]

        def split(src, hi, lo, *ready, on=None):
            t_hi = act.add(lambda e: e.activation(hi, src, ACT.Copy), *ready)
            t_lo = (on or dve).add(lambda e: e.tensor_tensor(lo, src, hi.bitcast(F32), ALU.subtract), t_hi, *ready)
            return t_lo

        def mm(out_ap, lhsT, rhs, start, stop, *waits, mark=False):
            return pe.add(lambda e: e.matmul(out_ap, lhsT, rhs, start=start, stop=stop), *waits, mark=mark)

        def mm3(out_ap, pairs, *waits, start=True, stop=True):
            pe.wait(*waits)
            n, last = 0, len(pairs) * len(PASSES) - 1
            for stat, mov in pairs:
                for a, b in PASSES:
                    t = mm(out_ap, stat[a], mov[b], start and n == 0, stop and n == last, mark=(n == last))
                    n += 1
            return t

        t_id0 = pool.add(lambda e: e.memset(ident[:], 0.0))
        t_ident = pool.add(lambda e: e.affine_select(out=ident[:], in_=ident[:], compare_op=ALU.not_equal, fill=1.0,
                                                     base=0, pattern=[[-1, P]], channel_multiplier=1), t_id0)
        t_half = pool.add(lambda e: e.memset(mneg_half[:], -0.5))

        ln_moments = {}

        def ln_tile(t):
            t_bn = dve.add(lambda e: e.bn_stats(ln_bn[:, t % 2, :], x[:, t, :]), x_ready[t])
            ln_moments[t] = dve.add(lambda e: e.bn_aggr(ln_mv[:, t, :], ln_bn[:, t % 2, :]), t_bn)

        def ln_inverse(tiles):
            a, b = tiles[0], tiles[-1] + 1
            t_v = pool.add(lambda e: e.tensor_scalar(ln_var[:, a:b], ln_mv[:, a:b, 1], LN_EPS, None, ALU.add),
                           [ln_moments[t] for t in tiles])
            return pool.add(lambda e: e.tensor_tensor(ln_rstd[:, a:b], ln_var[:, a:b], mneg_half[:, 0:b - a], ALU.pow),
                            t_v, t_half)

        def ln_stats(tiles):
            for t in tiles:
                ln_tile(t)
            return ln_inverse(tiles)

        xn_users = [None, None]
        turn = {"xn": 0}

        def ln_rows(t, t_rstd, xn):
            r = turn["xn"] % 2
            turn["xn"] += 1
            return r, dve.add(lambda e: e.tensor_scalar(xn[:, r, :], x[:, t, :], ln_mv[:, t, 0:1], ln_rstd[:, t:t + 1],
                                                        ALU.subtract, ALU.mult), t_rstd, xn_users[r])

        def ln_transpose(rows, xn, bank, hi, lo, *dst_free):
            r, t_xn = rows
            for k in range(KC):
                t_tr = pe.add(lambda e, k=k: e.transpose(psum[:, bank, k * P:(k + 1) * P], xn[:, r, k * P:(k + 1) * P],
                                                         ident[:]), t_xn, t_ident, bank_free[bank], mark=(k == KC - 1))
            xn_users[r] = t_tr
            src = psum[:, bank, :].rearrange("p (k c) -> p k c", k=KC)
            bank_free[bank] = split(src, hi, lo, t_tr, *dst_free)
            return bank_free[bank]

        def barrier(*others):
            marks = [l.now() for l in (pe, act, dve, pool)] + list(others)
            for l in (pe, act, dve, pool):
                l.wait(*marks)
            return marks

        phase1 = ExitStack()
        win_raw = sb("win_raw", [P, KC, DIM], F32, phase1)
        win_hi = sb("win_hi", [P, KC, 3 * DIM], F32R, phase1)
        win_lo = sb("win_lo", [P, KC, 3 * DIM], F32R, phase1)
        vec = sb("vec", [P, NVEC], F32, phase1)
        b1_sb = sb("b1_sb", [P, DEPTH, DFF // P], F32, phase1)
        w1_sb = sb("w1_sb", [P, DEPTH, DFF], F32, phase1)
        w2_sb = sb("w2_sb", [P, DEPTH * (DFF // P), 3 * DIM], F32, phase1)
        wout_sb = sb("wout_sb", [P, DM], F32, phase1)
        bout_sb = sb("bout_sb", [P, DM], F32, phase1)
        center = sb("center", [P, P], F32, phase1)
        blk_mean = sb("blk_mean", [P, NG2], F32, phase1)
        cosT = sb("cosT", [P, DEPTH, SEQ], F32, phase1)
        sinT = sb("sinT", [P, DEPTH, SEQ], F32, phase1)
        sm = sb("sm", [P, 32, DEPTH], F32, phase1)
        STEPS_APART = 6
        NS = NBLK
        SW = BLK // NG2
        SJ = SW // P
        h = [sb(f"h{i}", [P, SW], F32, phase1) for i in range(NS)]
        buf_a, buf_b, buf_c, buf_d, buf_e = ([sb(f"buf_{n}{i}", [P, SW], F32, phase1) for i in range(NS)] for n in "abcde")
        sl = sb("sl", [P, 2, DFF // P, NG2 * SW], F32, phase1)
        svar = sb("svar", [P, NS, SJ * NG2], F32, phase1)
        srstd = sb("srstd", [P, NS, SJ * NG2], F32, phase1)

        def ffn_buffers(stack, tag):
            d = {}
            d["xn"] = sb(f"xn{tag}", [P, 2, DM], F32, stack)
            d["xT"] = [[sb(f"xT{s}{part}{tag}", [P, KC, BLK], F32R, stack) for part in "hl"] for s in range(2)]
            d["wgu"] = [[sb(f"wgu{s}{part}{tag}", [P, 2 * DM], F32R, stack) for part in "hl"] for s in range(2)]
            d["wdn"] = [[sb(f"wdn{s}{part}{tag}", [P, DM], F32R, stack) for part in "hl"] for s in range(3)]
            d["gate"] = sb(f"gate{tag}", [P, 2, BLK], F32, stack)
            d["d"] = sb(f"d{tag}", [P, BLK], F32, stack)
            d["dT"] = [[sb(f"dT{s}{part}{tag}", [P, BLK], F32R, stack) for part in "hl"] for s in range(2)]
            d["raw"] = [stage[:, 0, :], stage[:, 1, :], sb(f"raw2{tag}", [P, 3 * DM], F32, stack)[:]]
            d["xT_free"] = [None, None]
            return d

        F1 = ffn_buffers(phase1, "a")
        LR_ROWS = 3 * RANK
        long_raw = sl[:].rearrange("p s n c -> p (s n c)")[:, 0:INNER]
        short_raw = stage[:, 1, :].rearrange("p (n d) -> p n d", n=3)
        tab = F1["gate"][:, 0, :].rearrange("p (l t) -> p l t", l=DEPTH)
        tab2 = F1["gate"][:, 1, :].rearrange("p (l t) -> p l t", l=DEPTH)
        long_st = sb("long_st", [P, INNER], F32R, phase1)
        short_st = sb("short_st", [P, 3, DM], F32R, phase1)

        s_vec = Slot(sem("vec_in"))
        for g in range(NG2):
            t_vec = s_vec.dma(sp, vec[g * DIM:(g + 1) * DIM, :], vecs)
        xv = x_in.rearrange("(t p) d -> p t d", p=P)
        for c in range(NBLK):
            t = Slot(sem(f"x_in{c}")).dma(sp, x[:, c * TPB:(c + 1) * TPB, :], xv[:, c * TPB:(c + 1) * TPB, :])
            for j in range(TPB):
                x_ready[c * TPB + j] = t
        t_zero_w2 = pool.add(lambda e: e.memset(w2_sb[:], 0.0))
        t_zero_short = pool.add(lambda e: e.memset(short_raw, 0.0))
        t_zero_long = dve.add(lambda e: e.memset(long_raw, 0.0))
        t_wz0 = dve.add(lambda e: e.memset(win_hi[:].bitcast(F32), 0.0))
        t_wz1 = dve.add(lambda e: e.memset(win_lo[:].bitcast(F32), 0.0))
        t_win = Slot(sem("win_in")).dma(act, win_raw[:], win.rearrange("(k p) d -> p k d", p=P))
        s_small = Slot(sem("small_in"))
        for g in range(NG2):
            rows = slice(g * DIM, (g + 1) * DIM)
            s_small.dma(act, w1_sb[rows, :, :], w1)
            s_small.dma(act, wout_sb[rows, :], wout)
        s_small.dma(act, b1_sb[:], b1)
        s_small.dma(act, bout_sb[:], bout.partition_broadcast(P))
        t_small = s_small.dma(act, w2_sb[:, :, DIM:2 * DIM], w2, t_zero_w2)
        s_lr = Slot(sem("lr_in"))
        for q in range(3):
            s_lr.dma(sp, long_raw[32 * q:32 * q + LR_ROWS, :], lr_long, t_zero_long)
            for kind in range(3):
                r = 32 * q + RANK * kind
                t_lr = s_lr.dma(sp, short_raw[r:r + RANK, kind, :], lr_short[RANK * kind:RANK * (kind + 1), :],
                                t_zero_short)

        t_c = pool.add(lambda e: e.memset(blk_mean[:], 0.0))
        t_c = pool.add(lambda e: e.memset(center[:], 0.0), t_c)
        for g in range(NG2):
            rows = slice(g * DIM, (g + 1) * DIM)
            pool.add(lambda e, r=rows, g=g: e.memset(blk_mean[r, g:g + 1], 1.0 / DIM), t_c)
            t_c2 = pool.add(lambda e, r=rows: e.memset(center[r, r], -1.0 / DIM), t_c)
        t_center = pool.add(lambda e: e.tensor_tensor(center[:], center[:], ident[:], ALU.add), t_c2, t_ident)

        def col(name, layer=None):
            a, w = VEC[name]
            return vec[:, a:a + w] if layer is None else vec[:, a + layer:a + layer + 1]

        cols = {n: i for i, n in enumerate(("m", "a", "b", "q", "z", "ri", "c1", "s1", "r", "rho", "t0", "t1", "t2",
                                            "mt", "za", "zb", "pc", "ps", "pc2", "ps2", "absi"))}

        def C(n):
            return sm[:, cols[n], :]

        def block_tiles(T):
            return list(range(T * TPB, (T + 1) * TPB))

        x_read = {}
        chain = [dve.add(lambda e: e.memset(sm[:], 0.0))]

        def step(lane, fn):
            chain[0] = lane.add(fn, chain[0])
            return chain[0]

        dve.wait(t_vec)
        step(dve, lambda e: e.tensor_scalar(C("m"), col("phz_re"), -1.0, None, ALU.mult))
        step(dve, lambda e: e.tensor_tensor(C("m"), C("m"), col("phz_re"), ALU.max))
        step(dve, lambda e: e.tensor_scalar(C("absi"), col("phz_im"), -1.0, None, ALU.mult))
        step(dve, lambda e: e.tensor_tensor(C("absi"), C("absi"), col("phz_im"), ALU.max))
        step(dve, lambda e: e.tensor_tensor(C("m"), C("m"), C("absi"), ALU.max))
        step(dve, lambda e: e.tensor_scalar(C("m"), C("m"), 1e-30, None, ALU.max))
        step(dve, lambda e: e.reciprocal(C("t0"), C("m")))
        step(dve, lambda e: e.tensor_tensor(C("a"), col("phz_re"), C("t0"), ALU.mult))
        step(dve, lambda e: e.tensor_tensor(C("b"), col("phz_im"), C("t0"), ALU.mult))
        step(dve, lambda e: e.tensor_tensor(C("q"), C("a"), C("a"), ALU.mult))
        step(dve, lambda e: e.tensor_tensor(C("t1"), C("b"), C("b"), ALU.mult))
        step(dve, lambda e: e.tensor_tensor(C("q"), C("q"), C("t1"), ALU.add))
        step(dve, lambda e: e.tensor_scalar(C("z"), C("q"), 0.0, None, ALU.is_equal))
        step(dve, lambda e: e.tensor_tensor(C("q"), C("q"), C("z"), ALU.add))
        step(dve, lambda e: e.tensor_tensor(C("a"), C("a"), C("z"), ALU.add))
        step(pool, lambda e: e.tensor_tensor(C("ri"), C("q"), mneg_half[:, 0:DEPTH], ALU.pow))
        rs0 = [ln_stats(block_tiles(0))]
        step(dve, lambda e: e.tensor_tensor(C("t0"), C("ri"), C("ri"), ALU.mult))
        step(dve, lambda e: e.tensor_tensor(C("t0"), C("t0"), C("q"), ALU.mult))
        step(dve, lambda e: e.tensor_scalar(C("t0"), C("t0"), -0.5, 1.5, ALU.mult, ALU.add))
        step(dve, lambda e: e.tensor_tensor(C("ri"), C("ri"), C("t0"), ALU.mult))
        step(dve, lambda e: e.tensor_tensor(C("c1"), C("a"), C("ri"), ALU.mult))
        step(dve, lambda e: e.tensor_tensor(C("s1"), C("b"), C("ri"), ALU.mult))
        step(dve, lambda e: e.tensor_tensor(C("r"), C("q"), C("ri"), ALU.mult))
        step(dve, lambda e: e.tensor_tensor(C("r"), C("r"), C("m"), ALU.mult))
        step(act, lambda e: e.activation(C("rho"), C("r"), ACT.Tanh))
        step(dve, lambda e: e.tensor_tensor(C("t0"), C("c1"), col("lc_re"), ALU.mult))
        step(dve, lambda e: e.tensor_tensor(C("t1"), C("s1"), col("lc_im"), ALU.mult))
        step(dve, lambda e: e.tensor_tensor(C("za"), C("t0"), C("t1"), ALU.subtract))
        step(dve, lambda e: e.tensor_tensor(C("t0"), C("c1"), col("lc_im"), ALU.mult))
        step(dve, lambda e: e.tensor_tensor(C("t1"), C("s1"), col("lc_re"), ALU.mult))
        step(dve, lambda e: e.tensor_tensor(C("zb"), C("t0"), C("t1"), ALU.add))
        step(dve, lambda e: e.tensor_scalar(C("zb"), C("zb"), -1.0, None, ALU.mult))
        t_state = chain[0]
        step(pool, lambda e: e.memset(cosT[:, :, 0:1], 1.0))
        step(pool, lambda e: e.memset(sinT[:, :, 0:1], 0.0))
        step(pool, lambda e: e.tensor_copy(C("pc"), C("c1")))
        step(pool, lambda e: e.tensor_copy(C("ps"), C("s1")))
        t_tables = []

        def tables():
            n = 1
            while n < SEQ:
                def wide(name, n=n):
                    return sm[:, cols[name], :].rearrange("p (l o) -> p l o", o=1).broadcast_to([P, DEPTH, n])
                c0, s0 = cosT[:, :, 0:n], sinT[:, :, 0:n]
                c1, s1 = cosT[:, :, n:2 * n], sinT[:, :, n:2 * n]
                ta, tb = tab[:, :, 0:n], tab2[:, :, 0:n]
                before = chain[0]
                pool.add(lambda e: e.tensor_tensor(c1, c0, wide("pc"), ALU.mult), before)
                p2 = pool.add(lambda e: e.tensor_tensor(ta, s0, wide("ps"), ALU.mult), before)
                pool.add(lambda e: e.tensor_tensor(s1, s0, wide("pc"), ALU.mult), before)
                p4 = pool.add(lambda e: e.tensor_tensor(tb, c0, wide("ps"), ALU.mult), before)
                pool.add(lambda e: e.tensor_tensor(c1, c1, ta, ALU.subtract), p2)
                chain[0] = pool.add(lambda e: e.tensor_tensor(s1, s1, tb, ALU.add), p4)
                n *= 2
                if n < SEQ:
                    step(pool, lambda e: e.tensor_tensor(C("pc2"), C("pc"), C("pc"), ALU.mult))
                    step(pool, lambda e: e.tensor_tensor(C("t1"), C("ps"), C("ps"), ALU.mult))
                    step(pool, lambda e: e.tensor_tensor(C("ps2"), C("pc"), C("ps"), ALU.mult))
                    step(pool, lambda e: e.tensor_tensor(C("pc"), C("pc2"), C("t1"), ALU.subtract))
                    step(pool, lambda e: e.tensor_tensor(C("ps"), C("ps2"), C("ps2"), ALU.add))
                else:
                    t_tables.append(chain[0])
                yield

        table_steps = tables()
        next(table_steps)

        t_winr = split(win_raw[:], win_hi[:, :, DIM:2 * DIM], win_lo[:, :, DIM:2 * DIM], t_win, t_wz0, t_wz1)
        t_lowrank = []

        def lowrank_split():
            t_l = act.add(lambda e: e.activation(long_st[0:96, :], long_raw[0:96, :], ACT.Copy), t_lr)
            yield
            t_s = act.add(lambda e: e.activation(short_st[0:96, :, :], short_raw[0:96, :, :], ACT.Copy), t_lr)
            yield
            dve.add(lambda e: e.tensor_tensor(long_st[32:64, :], long_raw[32:64, :], long_st[32:64, :].bitcast(F32),
                                              ALU.subtract), t_l)
            yield
            t_lowrank.append(dve.add(lambda e: e.tensor_tensor(short_st[64:96, :, :], short_raw[64:96, :, :],
                                                               short_st[64:96, :, :].bitcast(F32), ALU.subtract), t_s))
            stage_free[1] = t_lowrank[0]
            yield

        def set_up():
            for T in range(1, NBLK):
                for n in range(0, TPB, 2):
                    next(table_steps, None)
                    ln_tile(T * TPB + n)
                    ln_tile(T * TPB + n + 1)
                    if n + 2 == TPB:
                        rs0.append(ln_inverse(block_tiles(T)))
                    yield
            yield from table_steps
            yield from lowrank_split()

        hidden = [sl[:, 0], sl[:, 1], F1["gate"], F1["xn"]]
        last_hidden = [False] * NS
        hidden_free = [t_lowrank, t_lowrank, t_tables, None]

        def stack_stream(s):
            turn_b = [0]

            def bank():
                turn_b[0] += 1
                return 2 * s + turn_b[0] % 2

            hh, cen, sq, ur, yn, act_y = h[s], buf_a[s], buf_b[s], buf_c[s], buf_d[s], buf_e[s]
            zi, ui, rexp, zr = cen, sq, ur, yn
            tiles = list(range(s * TPB, (s + 1) * TPB))
            xT, hid = F1["xT"][s % 2], hidden[s]
            rows = {0: ln_rows(tiles[0], rs0[s], F1["xn"])}
            yield
            for j, t in enumerate(tiles):
                c_ = slice(j * P, (j + 1) * P)
                if j + 1 < TPB:
                    rows[j + 1] = ln_rows(t + 1, rs0[s], F1["xn"])
                t_x = ln_transpose(rows[j], F1["xn"], bank(), xT[0][:, :, c_], xT[1][:, :, c_], F1["xT_free"][s % 2])
                x_read[t] = rows[j][1]
                yield
            b = bank()
            pairs = []
            for g in range(NG2):
                w_off = DIM * (NG2 - 1 - g)
                pairs += [((win_hi[:, k, w_off:w_off + P], win_lo[:, k, w_off:w_off + P]),
                           (xT[0][:, k, g * SW:(g + 1) * SW], xT[1][:, k, g * SW:(g + 1) * SW])) for k in range(KC)]
            t_h = mm3(psum[:, b, 0:SW], pairs, t_x, t_winr, bank_free[b])
            F1["xT_free"][s % 2] = t_h
            rows_read = list(xn_users) if s == NS - 1 else None
            yield
            t_h = dve.add(lambda e: e.tensor_scalar(hh[:], psum[:, b, 0:SW], col("bin"), None, ALU.add), t_h, t_vec)
            bank_free[b] = t_h
            yield

            def norm(t_h):
                b = bank()
                t_c = mm(psum[:, b, 0:SW], center[:], hh[:], True, True, t_h, t_center, bank_free[b], mark=True)
                yield
                t_sq = act.add(lambda e: e.activation(sq[:], psum[:, b, 0:SW], ACT.Square), t_c)
                yield
                t_cc = dve.add(lambda e: e.tensor_copy(cen[:], psum[:, b, 0:SW]), t_sq)
                bank_free[b] = t_cc
                b = bank()
                for j in range(SJ):
                    t_v = mm(psum[:, b, j * NG2:(j + 1) * NG2], sq[:, j * P:(j + 1) * P], blk_mean[:], True, True,
                             t_sq, bank_free[b], mark=(j == SJ - 1))
                yield
                t_e = dve.add(lambda e: e.tensor_scalar(svar[:, s, :], psum[:, b, 0:SJ * NG2], LN_EPS, None, ALU.add), t_v)
                bank_free[b] = t_e
                t_r = pool.add(lambda e: e.tensor_tensor(srstd[:, s, :], svar[:, s, :], mneg_half[:, 0:SJ * NG2],
                                                         ALU.pow), t_e, t_half)
                yield
                t_x = dve.add(lambda e: e.tensor_copy(
                    rexp[:].rearrange("p (j d) -> p j d", d=DIM),
                    srstd[:, s, :].rearrange("p (j o) -> p j o", o=1).broadcast_to([P, SJ * NG2, DIM])), t_r)
                yield
                b = bank()
                for j in range(SJ):
                    t_t = pe.add(lambda e: e.transpose(psum[:, b, j * P:(j + 1) * P], rexp[:, j * P:(j + 1) * P],
                                                       ident[:]), t_x, bank_free[b], mark=(j == SJ - 1))
                yield
                t_y = dve.add(lambda e: e.tensor_tensor(yn[:], cen[:], psum[:, b, 0:SW], ALU.mult), t_t)
                bank_free[b] = t_y
                yield
                return t_y

            for l in range(DEPTH):
                t_y = yield from norm(t_h)
                if l == 0:
                    while not (t_tables and t_lowrank):
                        yield
                t_a = act.add(lambda e: e.activation(act_y[:], yn[:], ACT.Silu, bias=col("ln1_b", l),
                                                     scale=col("ln1_w", l)), t_y)
                yield
                cw, sw = cosT[:, l, :], sinT[:, l, :]
                t_ui = pool.add(lambda e: e.tensor_tensor(ui[:], act_y[:], sw, ALU.mult), t_a, t_tables)
                t_ur = dve.add(lambda e: e.tensor_tensor(ur[:], act_y[:], cw, ALU.mult), t_a, t_tables)
                yield
                rho = sm[:, cols["rho"], l:l + 1].broadcast_to([P, SW])
                t_zr = dve.add(lambda e: e.tensor_tensor_scan(zr[:], rho, ur[:], sm[:, cols["za"], l:l + 1],
                                                              ALU.mult, ALU.add), t_ur, t_state)
                t_zi = dve.add(lambda e: e.tensor_tensor_scan(zi[:], rho, ui[:], sm[:, cols["zb"], l:l + 1],
                                                              ALU.mult, ALU.add), t_ui, t_state)
                t_pi = pool.add(lambda e: e.tensor_tensor(ui[:], zi[:], sw, ALU.mult), t_zi)
                t_pr = dve.add(lambda e: e.tensor_tensor(ur[:], zr[:], cw, ALU.mult), t_zr)
                yield
                t_h = dve.add(lambda e: e.scalar_tensor_tensor(out=hh[:], in0=ur[:], scalar=col("sc_lin", l), in1=hh[:],
                                                               op0=ALU.mult, op1=ALU.add), t_pr)
                t_h = dve.add(lambda e: e.scalar_tensor_tensor(out=hh[:], in0=ui[:], scalar=col("sc_lin", l), in1=hh[:],
                                                               op0=ALU.mult, op1=ALU.add), t_h, t_pi)
                yield
                t_y = yield from norm(t_h)
                t_y2 = dve.add(lambda e: e.tensor_scalar(act_y[:], yn[:], col("ln2_w", l), col("ln2_b", l),
                                                         ALU.mult, ALU.add), t_y)
                t = tiles[l]
                x_ready[t] = pool.add(lambda e: e.tensor_tensor(x[:, t, :], x[:, t, :], bout_sb[:], ALU.add),
                                      x_read[t], t_small)
                yield
                t_sl = []
                banks2 = slice(2 * s, 2 * s + 2)
                for c in range(DFF // P):
                    for g in range(NG2):
                        rows = slice(g * DIM, (g + 1) * DIM)
                        t_m = mm(psum[:, 2 * s + g, c * SW:(c + 1) * SW], w1_sb[rows, l, c * P:(c + 1) * P],
                                 act_y[rows, :], True, True, t_y2, t_small, bank_free[2 * s], bank_free[2 * s + 1],
                                 mark=(c == DFF // P - 1))
                        last = [t_m] if g == 0 else last + [t_m]
                yield
                for c in range(DFF // P):
                    t_sl.append(act.add(lambda e: e.activation(
                        hid[:, c, :].rearrange("p (g t) -> p g t", g=NG2), psum[:, banks2, c * SW:(c + 1) * SW],
                        ACT.Silu, bias=b1_sb[:, l, c:c + 1]), last, hidden_free[s], rows_read))
                    yield
                bank_free[2 * s] = bank_free[2 * s + 1] = t_sl[-1]
                b = bank()
                n = 0
                for c in range(DFF // P):
                    for g in range(NG2):
                        off = DIM * (NG2 - 1 - g)
                        n += 1
                        t_m = mm(psum[:, b, 0:SW], w2_sb[:, l * (DFF // P) + c, off:off + P],
                                 hid[:, c, g * SW:(g + 1) * SW], n == 1, n == NG2 * (DFF // P), t_sl[c], bank_free[b],
                                 mark=(n == NG2 * (DFF // P)))
                hidden_free[s] = t_m
                last_hidden[s] = l == DEPTH - 1
                yield
                t_h = dve.add(lambda e: e.scalar_tensor_tensor(out=hh[:], in0=psum[:, b, 0:SW], scalar=col("b2", l),
                                                               in1=hh[:], op0=ALU.add, op1=ALU.add), t_m)
                bank_free[b] = t_h
                yield
            t_y = yield from norm(t_h)
            t_y2 = dve.add(lambda e: e.tensor_scalar(act_y[:], yn[:], col("lnl_w"), col("lnl_b"), ALU.mult, ALU.add),
                           t_y)
            yield
            for n, t in enumerate(tiles):
                g, j = divmod(n, SJ)
                rows = slice(g * DIM, (g + 1) * DIM)
                b = bank()
                t_m = mm(psum[:, b, :], act_y[rows, j * P:(j + 1) * P], wout_sb[rows, :], True, True, t_y2,
                         bank_free[b], mark=True)
                yield
                x_ready[t] = dve.add(lambda e: e.tensor_tensor(x[:, t, :], x[:, t, :], psum[:, b, :], ALU.add),
                                     t_m, x_ready[t])
                bank_free[b] = x_ready[t]
            yield

        GATE, UP, AUX, DOWN = 2, 3, (0, 1), 4
        weff_slot = [Slot(sem(f"weff_out{i}")) for i in range(2)]
        weff_saved = [None] * IC

        aux_turn = [0]

        def aux_bank():
            aux_turn[0] += 1
            return AUX[aux_turn[0] % 2]

        def ffn(F, make_weff, prep, first_norm, buffers_free=None, finished=None, last_steps=None, raw_first=0,
                loaded=None):
            nseq = NBLK * IC
            wgu_free, wdn_free = [None] * 2, [None] * 3
            gate_free, dT_free = [buffers_free] * 2, [None, None]
            d_free = [None]

            def fetch(n):
                T, i = divmod(n, IC)
                src = ffn_w[i] if make_weff and T == 0 else weff_dram[i]
                r = (n + raw_first) % 3
                return stage_slot[r].dma(sp, F["raw"][r], src, stage_free[r],
                                         None if make_weff and T == 0 else weff_saved[i])

            t_gu, t_dn = {}, {}

            def weights(n, t_raw):
                T, i = divmod(n, IC)
                r, s, sd = (n + raw_first) % 3, n % 2, n % 3
                raw = F["raw"][r]

                def split_gu(*w):
                    t_gu[n] = split(raw[:, 0:2 * DM], F["wgu"][s][0][:], F["wgu"][s][1][:], *w, wgu_free[s])

                def split_dn(*w):
                    t_dn[n] = split(raw[:, 2 * DM:], F["wdn"][sd][0][:], F["wdn"][sd][1][:], *w, wdn_free[sd])
                    stage_free[r] = [t_gu[n], t_dn[n]]

                def scale(kind):
                    b = aux_bank()
                    cols_ = slice(i * P, (i + 1) * P)
                    pe.wait(bank_free[b], t_lowrank)
                    if kind < 2:
                        for k in range(KC):
                            t_m = mm(psum[:, b, k * P:(k + 1) * P], short_st[0:96, kind, k * P:(k + 1) * P],
                                     long_st[0:96, cols_], True, True, mark=(k == KC - 1))
                    else:
                        t_m = mm(psum[:, b, :], long_st[0:96, cols_], short_st[0:96, kind, :], True, True, mark=True)
                    part = raw[:, kind * DM:(kind + 1) * DM]
                    bank_free[b] = dve.add(lambda e: e.tensor_tensor(part, part, psum[:, b, :], ALU.mult), t_m, t_raw)
                    return bank_free[b]

                if not (make_weff and T == 0):
                    split_gu(t_raw)
                    yield
                    split_dn(t_raw)
                    return
                scale(0)
                yield
                split_gu(scale(1))
                yield
                t_w = scale(2)
                split_dn(t_w)
                weff_saved[i] = weff_slot[i % 2].dma(sp, weff_dram[i], raw, t_w, weff_saved[i - 2] if i >= 2 else None)
                stage_free[r] = [t_gu[n], t_dn[n], weff_saved[i]]

            t_raw = loaded or {n: fetch(n) for n in range(2)}
            yield
            for _ in weights(0, t_raw[0]):
                yield
            yield
            t_xT = first_norm()
            down = None
            for T in range(NBLK):
                xT = F["xT"][T % 2]
                ahead = prep(T + 1)
                t_next = None
                for i in range(IC):
                    n = T * IC + i
                    s = n % 2
                    w, wd = F["wgu"][s], F["wdn"][n % 3]
                    if n + 2 < nseq:
                        t_raw[n + 2] = fetch(n + 2)
                    elif n + 2 == nseq and last_steps:
                        last_steps()
                    following = weights(n + 1, t_raw[n + 1]) if n + 1 < nseq else iter(())
                    for bank_, off in ((GATE, 0), (UP, DM)):
                        next(following, None)
                        pairs = [((w[0][:, off + k * P:off + (k + 1) * P], w[1][:, off + k * P:off + (k + 1) * P]),
                                  (xT[0][:, k, :], xT[1][:, k, :])) for k in range(KC)]
                        t_m = mm3(psum[:, bank_, :], pairs, t_gu[n], t_xT, bank_free[bank_])
                        if bank_ == GATE:
                            t_g = act.add(lambda e, s=s: e.activation(F["gate"][:, s, :], psum[:, GATE, :], ACT.Silu),
                                          t_m, gate_free[s])
                            bank_free[GATE] = t_g
                            yield
                    if i == IC - 1:
                        F["xT_free"][T % 2] = t_m
                    wgu_free[s] = t_m
                    t_d = dve.add(lambda e, s=s: e.tensor_tensor(F["d"][:], F["gate"][:, s, :], psum[:, UP, :], ALU.mult),
                                  t_m, t_g, d_free[0])
                    bank_free[UP] = t_d
                    gate_free[s] = t_d
                    t_ds = split(F["d"][:], F["dT"][s][0][:], F["dT"][s][1][:], t_d, dT_free[s])
                    d_free[0] = t_ds
                    next(following, None)
                    yield
                    if down:
                        down()

                    def down(T=T, i=i, s=s, t_ds=t_ds, wd=wd, sd=n % 3, t_wd=t_dn[n]):
                        for j in range(TPB):
                            c_ = slice(j * P, (j + 1) * P)
                            pairs = [((F["dT"][s][0][:, c_], F["dT"][s][1][:, c_]), (wd[0][:], wd[1][:]))]
                            t_m = mm3(psum[:, DOWN + j, :], pairs, t_ds, t_wd, bank_free[DOWN + j] if i == 0 else None,
                                      start=(i == 0), stop=(i == IC - 1))
                            if i == IC - 1:
                                t = T * TPB + j
                                x_ready[t] = dve.add(lambda e, t=t, j=j: e.tensor_tensor(
                                    x[:, t, :], x[:, t, :], psum[:, DOWN + j, :], ALU.add), t_m, x_ready[t])
                                bank_free[DOWN + j] = x_ready[t]
                        wdn_free[sd] = dT_free[s] = t_m
                        if i == IC - 1 and finished:
                            finished(T)
                    if t_next is None:
                        try:
                            next(ahead)
                        except StopIteration as stop:
                            t_next = stop.value
                    yield
                while t_next is None and T + 1 < NBLK:
                    try:
                        next(ahead)
                    except StopIteration as stop:
                        t_next = stop.value
                t_xT = t_next
            down()

        def block_norm(F, T, xn=None, rs=None):
            tiles = block_tiles(T)
            if xn is None:
                xn = F["xn"]
            if rs is None:
                for t in tiles:
                    ln_tile(t)
                    if t % 2:
                        yield
                rs = ln_inverse(tiles)
            xT = F["xT"][T % 2]
            rows = {0: ln_rows(tiles[0], rs, xn)}
            yield
            for j, t in enumerate(tiles):
                c_ = slice(j * P, (j + 1) * P)
                if j + 1 < TPB:
                    rows[j + 1] = ln_rows(t + 1, rs, xn)
                t_x = ln_transpose(rows[j], xn, aux_bank(), xT[0][:, :, c_], xT[1][:, :, c_], F["xT_free"][T % 2])
                yield
            return t_x

        def in_turn(*streams):
            live, turn = list(streams), 0
            while live:
                for entry in list(live):
                    if turn >= entry[0] and next(entry[1], "end") == "end":
                        live.remove(entry)
                turn += 1

        first_block = []
        done = [False] * NS
        gate_free_first = []

        def stream(s):
            yield from stack_stream(s)
            done[s] = True

        def ffn_start():
            while not t_lowrank:
                yield
            next(ffn1)
            while not done[0]:
                yield
            xn_users[:] = [hidden_free[0]] * 2
            norm = block_norm(F1, 0, xn=hidden[0])
            for part in range(3):
                if part > 0:
                    next(norm)
                    yield
                next(ffn1)
                yield
            first_block.append((yield from norm))
            while not (done[1] and last_hidden[2]):
                yield
            gate_free_first.append(hidden_free[2])
            next(ffn1)
            yield

        rs_att = {}

        def norm_and_stats(T):
            t_x = (yield from block_norm(F1, T)) if T < NBLK else None
            if T >= 2:
                for t in block_tiles(T - 2):
                    ln_tile(t)
                    yield
                rs_att[T - 2] = ln_inverse(block_tiles(T - 2))
            return t_x

        KVQ = 2 * HD + GRP * HD

        def load_halves(src):
            half = src.shape[-1] // 2
            return [stage_slot[n].dma(sp, stage[:, n, 0:half], src[:, n * half:(n + 1) * half], stage_free[n])
                    for n in range(2)]

        kvq_first = []
        ffn1 = ffn(F1, True, norm_and_stats, lambda: first_block[0], buffers_free=gate_free_first, raw_first=1,
                   last_steps=lambda: kvq_first.extend(load_halves(wqkv[0])))
        in_turn((0, set_up()), *((s_ * STEPS_APART, stream(s_)) for s_ in range(NS)), (0, ffn_start()))
        xn_users[:] = [hidden_free[3]] * 2
        for _ in ffn1:
            pass

        t_kvq_raw = kvq_first
        marks = barrier(*weff_saved)
        phase1.close()

        phase2 = ExitStack()

        def sb2(name, shape, dt=F32):
            return sb(name, shape, dt, phase2)
        axT = [sb2(f"axT_{p}", [P, KC, TOK], F32R) for p in "hl"]
        wkvq = [sb2(f"wkvq_{p}", [P, KC, KVQ], F32R) for p in "hl"]
        wo_s = [sb2(f"wo_{p}", [P, GRP, DM], F32R) for p in "hl"]
        qT = [sb2(f"qT_{p}", [P, GRP, SEQ], F32R) for p in "hl"]
        kT = [sb2(f"kT_{p}", [P, SEQ], F32R) for p in "hl"]
        vv = [[sb2(f"v{s}_{p}", [P, STILES, HD], F32R) for p in "hl"] for s in range(2)]
        oT = [sb2(f"oT_{p}", [P, GRP, SEQ], F32R) for p in "hl"]
        q_tok = sb2("q_tok", [P, STILES, GRP * HD])
        k_tok = sb2("k_tok", [P, STILES, HD])
        squares = sb2("squares", [P, GRP * HD])
        SC = P + SEQ
        biased = sb2("biased", [P, 2, SC])
        prob = sb2("prob", [P, GRP, SC])
        pT = [sb2(f"pT_{p}", [P, 2, SC], F32R) for p in "hl"]
        xn_a = sb2("xn_a", [P, DM])
        alibi = sb2("alibi", [P, GRP, SC])
        rel = sb2("rel", [P, SC])
        future = sb2("future", [P, SC])
        qkw = sb2("qkw", [P, 2, HD])
        kw = sb2("kw", [P, HD])
        ss_q = sb2("ss_q", [P, STILES, GRP])
        r_q = sb2("r_q", [P, STILES, GRP])
        ss_k = sb2("ss_k", [P, STILES])
        r_k = sb2("r_k", [P, STILES])
        nmax = sb2("nmax", [P, GRP, STILES])
        esum = sb2("esum", [P, GRP, STILES])
        rsum = sb2("rsum", [P, GRP, STILES])
        KV, QB, WO = 4, (5, 6), 7

        t_qkw = Slot(sem("qkw_in")).dma(sp, qkw[:], qk_w.partition_broadcast(P), marks)
        ready_w = {}
        free_w = {"kv": None, "q": None, "wo": None}

        def split_kv(t_raw, on=pool):
            src = stage[:].rearrange("p a (k n) -> p (a k) n", n=KVQ)[:, :, 0:2 * HD]
            ready_w["kv"] = split(src, wkvq[0][:, :, 0:2 * HD], wkvq[1][:, :, 0:2 * HD], t_raw, free_w["kv"], on=on)

        def split_q(half, t_raw, on=pool):
            k = slice(half * KC // 2, (half + 1) * KC // 2)
            src = stage[:, half, :].rearrange("p (k n) -> p k n", n=KVQ)[:, :, 2 * HD:]
            ready_w["q", half] = split(src, wkvq[0][:, k, 2 * HD:], wkvq[1][:, k, 2 * HD:], t_raw[half], free_w["q"], on=on)
            stage_free[half] = [ready_w["kv"], ready_w["q", half]]

        def split_wo(half, t_raw):
            hs = slice(half * GRP // 2, (half + 1) * GRP // 2)
            src = stage[:, half, 0:GRP // 2 * DM].rearrange("p (h n) -> p h n", n=DM)
            ready_w["wo", half] = split(src, wo_s[0][:, hs, :], wo_s[1][:, hs, :], t_raw[half], free_w["wo"], on=pool)
            stage_free[half] = ready_w["wo", half]

        t_ax = [None] * NT
        xn_read = [None]
        t_xn = [None]

        def norm_rows(t):
            t_xn[0] = dve.add(lambda e: e.tensor_scalar(xn_a[:], x[:, t, :], ln_mv[:, t, 0:1], ln_rstd[:, t:t + 1],
                                                        ALU.subtract, ALU.mult), rs_att[t // TPB], xn_read[0])

        def norm_transpose(t, bank=WO):
            for k in range(KC):
                t_tr = pe.add(lambda e: e.transpose(psum[:, bank, k * P:(k + 1) * P], xn_a[:, k * P:(k + 1) * P],
                                                    ident[:]), t_xn[0], bank_free[bank], mark=(k == KC - 1))
            xn_read[0] = t_tr
            c_ = slice(t * P, (t + 1) * P)
            t_ax[t] = bank_free[bank] = split(psum[:, bank, :].rearrange("p (k c) -> p k c", k=KC),
                                              axT[0][:, :, c_], axT[1][:, :, c_], t_tr)

        t_al, al_free = [None] * GRP, [None] * GRP

        def alibi_table(g, hd):
            t_al[hd] = dve.add(lambda e: e.scalar_tensor_tensor(
                out=alibi[:, hd, :], in0=rel[:], scalar=SLOPES[g * GRP + hd], in1=future[:],
                op0=ALU.mult, op1=ALU.add), t_fut, al_free[hd])

        ft = {"v": [None, None], "kT": None, "qT": None, "k_tok": None, "q_tok": [None, None], "oT": None,
              "biased": [None, None], "prob": [None] * GRP, "pT": None, "sq": None}
        tk = {}

        def kv_proj(u):
            g, b = divmod(u, BATCH)
            s = u % 2
            for t in range(STILES):
                tile = b * STILES + t
                c_ = slice(tile * P, (tile + 1) * P)
                pairs = [((axT[0][:, k, c_], axT[1][:, k, c_]), (wkvq[0][:, k, 0:2 * HD], wkvq[1][:, k, 0:2 * HD]))
                         for k in range(KC)]
                t_m = mm3(psum[:, KV, t * 2 * HD:(t + 1) * 2 * HD], pairs, t_ax[tile], ready_w["kv"], bank_free[KV])
            if b == BATCH - 1:
                free_w["kv"] = t_m
            kv = psum[:, KV, :].rearrange("p (t n) -> p t n", t=STILES)
            for t in range(STILES):
                t_ss = act.add(lambda e, t=t: e.activation(squares[:, t * HD:(t + 1) * HD], kv[:, t, 0:HD], ACT.Square,
                                                           accum_out=ss_k[:, t:t + 1]), t_m, ft["sq"], ft["k_tok"])
            ft["sq"] = t_ss
            t_a = pool.add(lambda e: e.tensor_scalar(ss_k[:], ss_k[:], 1.0 / HD, RMS_EPS, ALU.mult, ALU.add), t_ss)
            t_r = pool.add(lambda e: e.tensor_tensor(r_k[:], ss_k[:], mneg_half[:, 0:STILES], ALU.pow), t_a)
            tk["v"] = split(kv[:, :, HD:2 * HD], vv[s][0][:], vv[s][1][:], t_m, ft["v"][s])
            tk["kr"] = t_r

        def k_scale(u):
            kv = psum[:, KV, :].rearrange("p (t n) -> p t n", t=STILES)
            for t in range(STILES):
                t_k = dve.add(lambda e, t=t: e.scalar_tensor_tensor(out=k_tok[:, t, :], in0=kv[:, t, 0:HD],
                                                                    scalar=r_k[:, t:t + 1], in1=kw[:], op0=ALU.mult,
                                                                    op1=ALU.mult), tk["kr"], t_kw, ft["k_tok"])
            bank_free[KV] = [tk["v"], t_k]
            tk["k"] = t_k

        def k_transpose(u):
            for t in range(STILES):
                t_t = pe.add(lambda e, t=t: e.transpose(psum[:, KV, t * P:(t + 1) * P], k_tok[:, t, :], ident[:]),
                             tk["k"], bank_free[KV], mark=(t == STILES - 1))
            ft["k_tok"] = t_t
            tk["kT"] = bank_free[KV] = split(psum[:, KV, 0:SEQ], kT[0][:], kT[1][:], t_t, ft["kT"])

        def q_proj(u, t):
            g, b = divmod(u, BATCH)
            tile = b * STILES + t
            c_ = slice(tile * P, (tile + 1) * P)
            for half in range(2):
                pairs = [((axT[0][:, k, c_], axT[1][:, k, c_]), (wkvq[0][:, k, 2 * HD:], wkvq[1][:, k, 2 * HD:]))
                         for k in range(half * KC // 2, (half + 1) * KC // 2)]
                t_m = mm3(psum[:, QB[t], :], pairs, t_ax[tile], ready_w["q", half], bank_free[QB[t]],
                          start=(half == 0), stop=(half == 1))
            if b == BATCH - 1:
                free_w["q"] = t_m
            t_sq = act.add(lambda e: e.activation(squares[:], psum[:, QB[t], :], ACT.Square), t_m, ft["sq"])
            t_ss = dve.add(lambda e: e.tensor_reduce(ss_q[:, t, :], squares[:].rearrange("p (h d) -> p h d", h=GRP),
                                                     AX.X, ALU.add), t_sq, ft["q_tok"][t])
            ft["sq"] = t_ss
            t_a = pool.add(lambda e: e.tensor_scalar(ss_q[:, t, :], ss_q[:, t, :], 1.0, HD * RMS_EPS, ALU.mult, ALU.add),
                           t_ss)
            t_r = pool.add(lambda e: e.tensor_tensor(r_q[:, t, :], ss_q[:, t, :], mneg_half[:, 0:GRP], ALU.pow), t_a)
            tk["qr", t] = t_r

        def q_scale(u, t):
            t_q = dve.add(lambda e: e.tensor_tensor(
                q_tok[:, t, :].rearrange("p (h d) -> p h d", h=GRP),
                psum[:, QB[t], :].rearrange("p (h d) -> p h d", h=GRP),
                r_q[:, t, :].rearrange("p (h o) -> p h o", o=1).broadcast_to([P, GRP, HD]), ALU.mult),
                tk["qr", t], ft["q_tok"][t])
            bank_free[QB[t]] = t_q
            tk["q", t] = t_q

        def q_transpose(u, t):
            for hd in range(GRP):
                t_t = pe.add(lambda e, hd=hd: e.transpose(psum[:, QB[t], hd * P:(hd + 1) * P],
                                                          q_tok[:, t, hd * HD:(hd + 1) * HD], ident[:]),
                             tk["q", t], bank_free[QB[t]], mark=(hd == GRP - 1))
            ft["q_tok"][t] = t_t
            c_ = slice(t * P, (t + 1) * P)
            tk["qT", t] = bank_free[QB[t]] = split(psum[:, QB[t], :].rearrange("p (h c) -> p h c", h=GRP),
                                                   qT[0][:, :, c_], qT[1][:, :, c_], t_t, ft["qT"])

        def scores(u, hd):
            s = hd % 2
            part = ((0, P), (P, SC))
            for t in range(STILES):
                a, b_ = part[t]
                q_ = slice(t * P, (t + 1) * P)
                pairs = [((qT[0][:, hd, q_], qT[1][:, hd, q_]), (kT[0][:, 0:b_ - a], kT[1][:, 0:b_ - a]))]
                t_m = mm3(psum[:, hd, a:b_], pairs, tk["qT", t], tk["kT"], bank_free[hd])
            ft["qT"] = ft["kT"] = t_m
            for t in range(STILES):
                a, b_ = part[t]
                t_b = dve.add(lambda e, t=t, a=a, b_=b_: e.tensor_tensor_reduce(
                    biased[:, s, a:b_], psum[:, hd, a:b_], alibi[:, hd, a:b_], -1.0, 3e38, ALU.add, ALU.min,
                    nmax[:, hd, t:t + 1]), t_m, t_al[hd], ft["biased"][s])
                t_e = act.add(lambda e, t=t, a=a, b_=b_: e.activation(
                    prob[:, hd, a:b_], biased[:, s, a:b_], ACT.Exp, bias=nmax[:, hd, t:t + 1], scale=-1.0,
                    accum_out=esum[:, hd, t:t + 1]), t_b, ft["prob"][hd])
            bank_free[hd] = al_free[hd] = t_b
            ft["biased"][s] = tk["e", hd] = t_e

        def normalise(hd):
            part = ((0, P), (P, SC))
            t_r = dve.add(lambda e: e.reciprocal(rsum[:, hd, :], esum[:, hd, :]), tk["e", hd])
            for t in range(STILES):
                a, b_ = part[t]
                t_p = pool.add(lambda e, t=t, a=a, b_=b_: e.tensor_scalar(prob[:, hd, a:b_], prob[:, hd, a:b_],
                                                                          rsum[:, hd, t:t + 1], 1.0, ALU.mult, ALU.mult), t_r)
            tk["p", hd] = t_p

        def p_transpose(u, hd):
            s = hd % 2
            for n in range(SC // P):
                t_t = pe.add(lambda e: e.transpose(psum[:, hd, n * P:(n + 1) * P], prob[:, hd, n * P:(n + 1) * P],
                                                   ident[:]), tk["p", hd], bank_free[hd], mark=(n == SC // P - 1))
            ft["prob"][hd] = t_t
            tk["pT", hd] = bank_free[hd] = split(psum[:, hd, 0:SC], pT[0][:, s, :], pT[1][:, s, :], t_t, ft["pT"])

        def attend(u, pair):
            v = vv[u % 2]
            b = 2 * pair
            both = psum[:, b, :].rearrange("p (h c) -> p h c", h=2)
            mm3(both, [((v[0][:, 0, :], v[1][:, 0, :]), (pT[0][:, :, 0:SEQ], pT[1][:, :, 0:SEQ]))],
                tk["pT", b], tk["pT", b + 1], tv[u % 2], bank_free[b], stop=False)
            t_m = mm3(both[:, :, P:SEQ], [((v[0][:, 1, :], v[1][:, 1, :]), (pT[0][:, :, SEQ:], pT[1][:, :, SEQ:]))],
                      start=False)
            ft["pT"] = t_m
            ft["v"][u % 2] = t_m
            tk["oT", pair] = bank_free[b] = split(both, oT[0][:, b:b + 2, :], oT[1][:, b:b + 2, :], t_m, ft["oT"])

        def out_proj(u, t):
            g, b = divmod(u, BATCH)
            tile = b * STILES + t
            c_ = slice(t * P, (t + 1) * P)
            bank = (1, WO)[t]
            pe.wait(bank_free[bank])
            for hd in range(GRP):
                t_m = mm3(psum[:, bank, :], [((oT[0][:, hd, c_], oT[1][:, hd, c_]), (wo_s[0][:, hd, :], wo_s[1][:, hd, :]))],
                          tk["oT", hd // 2], ready_w["wo", hd // (GRP // 2)], start=(hd == 0), stop=(hd == GRP - 1))
            if t == STILES - 1:
                ft["oT"] = t_m
                if b == BATCH - 1:
                    free_w["wo"] = t_m
            x_ready[tile] = dve.add(lambda e: e.tensor_tensor(x[:, tile, :], x[:, tile, :], psum[:, bank, :], ALU.add),
                                    t_m, x_ready[tile])
            bank_free[bank] = x_ready[tile]

        tv = [None, None]
        units = KVH * BATCH
        ahead = 2
        norm_rows(0)
        split_kv(t_kvq_raw, on=dve)
        norm_transpose(0, QB[0])
        norm_rows(1)
        split_q(1, t_kvq_raw)
        norm_transpose(1, QB[1])
        split_q(0, t_kvq_raw, on=dve)
        t_kw = dve.add(lambda e: e.tensor_tensor(kw[:], qkw[:, 0, :], qkw[:, 1, :], ALU.mult), t_qkw)
        kv_proj(0)
        tv[0] = tk["v"]
        k_scale(0)
        t_wo_raw = load_halves(wo[0])
        pool.add(lambda e: e.iota(rel[:, 0:P], [[1, P]], base=0, channel_multiplier=-1,
                                  allow_small_or_imprecise_dtypes=True))
        t_rel = pool.add(lambda e: e.iota(rel[:, P:], [[1, SEQ]], base=-P, channel_multiplier=-1,
                                          allow_small_or_imprecise_dtypes=True))
        for t in range(STILES):
            q_proj(0, t)
            norm_rows(STILES + t)
            norm_transpose(STILES + t)
            q_scale(0, t)
        k_transpose(0)
        for t in range(STILES):
            q_transpose(0, t)
        t_fut = dve.add(lambda e: e.tensor_scalar(future[:], rel[:], 0.0, NEG_INF, ALU.is_gt, ALU.mult), t_rel)
        for hd in range(GRP):
            alibi_table(0, hd)
        for u in range(units):
            g, b = divmod(u, BATCH)
            nxt = u + 1 < units
            if u < TPB:
                ln_tile(NT - TPB + u)
                if u == TPB - 1:
                    rs_att[NBLK - 1] = ln_inverse(block_tiles(NBLK - 1))
            if u == units - 4:
                rs_next = ln_stats(block_tiles(0))
                loaded = {n: stage_slot[n].dma(sp, stage[:, n, :], weff_dram[n], stage_free[n], weff_saved[n])
                          for n in range(2)}
            last_proj = b == BATCH - 2 and g + 1 < KVH
            fresh = [t for t in range((u + ahead) * STILES, (u + ahead + 1) * STILES) if t < NT]
            for hd in range(GRP):
                scores(u, hd)
                if b == BATCH - 1 and nxt:
                    alibi_table(g + 1, hd)
                if hd > 0:
                    normalise(hd - 1)
            normalise(GRP - 1)
            if fresh:
                norm_rows(fresh[0])
            if nxt:
                kv_proj(u + 1)
                tv[(u + 1) % 2] = tk["v"]
            if b == 0:
                split_wo(0, t_wo_raw)
            p_transpose(u, 0)
            p_transpose(u, 1)
            if nxt:
                k_scale(u + 1)
            if fresh:
                norm_transpose(fresh[0])
                norm_rows(fresh[1])
            if nxt:
                q_proj(u + 1, 0)
            if last_proj:
                split_kv(t_kvq_raw)
            if b == 0:
                split_wo(1, t_wo_raw)
                if g + 1 < KVH:
                    t_kvq_raw = load_halves(wqkv[g + 1])
            attend(u, 0)
            p_transpose(u, 2)
            p_transpose(u, 3)
            if nxt:
                q_scale(u + 1, 0)
            if fresh:
                norm_transpose(fresh[1])
            if nxt:
                q_proj(u + 1, 1)
            if last_proj:
                split_q(0, t_kvq_raw)
            attend(u, 1)
            if nxt:
                q_scale(u + 1, 1)
                k_transpose(u + 1)
                q_transpose(u + 1, 0)
            if last_proj:
                split_q(1, t_kvq_raw)
                t_wo_raw = load_halves(wo[g + 1])
            out_proj(u, 0)
            if nxt:
                q_transpose(u + 1, 1)
            out_proj(u, 1)
        attention_over = barrier()
        phase2.close()

        phase3 = ExitStack()
        F2 = ffn_buffers(phase3, "b")
        xn_users[:] = [None, None]
        ov = out.rearrange("(t p) d -> p t d", p=P)
        stored = []
        stage_free[2] = attention_over

        def store(T):
            tiles = range(T * TPB, (T + 1) * TPB)
            if T < NBLK - 1:
                stored.append(Slot(sem(f"x_out{T}")).dma(
                    sp, ov[:, tiles[0]:tiles[-1] + 1, :], x[:, tiles[0]:tiles[-1] + 1, :], x_ready[tiles[-1]]))
            else:
                for t in tiles:
                    stored.append(Slot(sem(f"x_out_tile{t}")).dma(sp, ov[:, t, :], x[:, t, :], x_ready[t]))

        def first_norm():
            norm = block_norm(F2, 0, rs=rs_next)
            while True:
                try:
                    next(norm)
                except StopIteration as stop:
                    return stop.value

        for _ in ffn(F2, False, lambda T: block_norm(F2, T) if T < NBLK else iter(()), first_norm, finished=store,
                     loaded=loaded):
            pass
        sp.wait(*stored)
        phase3.close()


def kernel(**inputs):
    import concourse.bacc as bacc
    from concourse.bass_utils import run_bass_kernel_spmd

    a = {n[3:]: np.asarray(v) for n, v in inputs.items()}
    x = a["attn_a_x"].reshape(TOK, DM)
    win = a["attn_a_Win"].T
    vecs = np.concatenate([a["attn_a_" + n].T.reshape(DIM, w) for n, (_, w) in VEC.items()], axis=1)
    b1 = a["attn_a_b1"].reshape(DEPTH, DFF // P, P).transpose(2, 0, 1)
    w1 = a["attn_a_W1"].transpose(2, 0, 1)
    w2 = a["attn_a_W2"].transpose(0, 2, 1).reshape(DEPTH, DFF // P, P, DIM).transpose(2, 0, 1, 3).reshape(P, -1, DIM)
    wout = a["attn_a_Wout"].T

    def in_out(w):
        return w.reshape(IC, P, KC, P).transpose(0, 3, 2, 1).reshape(IC, P, DM)
    ffn_w = np.concatenate([in_out(a["ffn_gate_w"]), in_out(a["ffn_up_w"]),
                            a["ffn_down_w"].T.reshape(IC, P, DM)], axis=2)
    lr_long = np.concatenate([a["ffn_gate_su"].T, a["ffn_up_su"].T, a["ffn_down_sv"]], axis=0)
    lr_short = np.concatenate([a["ffn_gate_sv"], a["ffn_up_sv"], a["ffn_down_su"].T], axis=0)

    def by_group(w, n):
        return w.reshape(KVH, n, KC, P).transpose(0, 3, 2, 1)
    wqkv = np.concatenate([by_group(a["attn_b_Wk"], HD), by_group(a["attn_b_Wv"], HD),
                           by_group(a["attn_b_Wq"], GRP * HD)], axis=3).reshape(KVH, P, -1)
    wo = a["attn_b_Wo"].reshape(DM, KVH, GRP, HD).transpose(1, 3, 2, 0).reshape(KVH, HD, -1)
    qk_w = np.stack([a["attn_b_q_norm_w"], a["attn_b_k_norm_w"]])

    nc = bacc.Bacc("TRN2", target_bir_lowering=False, num_devices=1)
    arrays, args = {}, []
    for name, v in (("x", x), ("win", win), ("vecs", vecs), ("b1", b1), ("w1", w1), ("w2", w2), ("wout", wout),
                    ("bout", a["attn_a_bout"]), ("ffn_w", ffn_w), ("lr_long", lr_long), ("lr_short", lr_short),
                    ("wqkv", wqkv), ("wo", wo), ("qk_w", qk_w)):
        name = "in_" + name
        arrays[name] = np.ascontiguousarray(v)
        args.append(nc.dram_tensor(name, arrays[name].shape, F32, kind="ExternalInput").ap())
    args.append(nc.dram_tensor("out", (TOK, DM), F32, kind="ExternalOutput").ap())
    args.append(nc.dram_tensor("weff_dram", (IC, P, 3 * DM), F32, kind="Internal").ap())
    hybrid_block(nc, *args)
    r = run_bass_kernel_spmd(nc, [arrays], core_ids=[0])
    return r.results[0]["out"].reshape(BATCH, SEQ, DM)
```
